# Optimizing a Trainium2 kernel written in Bass

```python
import numpy as np
import jax
import jax.numpy as jnp

def _softmax(x, axis=-1):
    return jax.nn.softmax(x, axis=axis)

def _gelu(x):
    return jax.nn.gelu(x, approximate=True)

def _silu(x):
    return jax.nn.silu(x)

def _sigmoid(x):
    return jax.nn.sigmoid(x)

def _layernorm(x, axis=-1, eps=1e-05):
    m = jnp.mean(x, axis=axis, keepdims=True)
    v = jnp.var(x, axis=axis, keepdims=True)
    return (x - m) / jnp.sqrt(v + eps)

def _scatter_add(tgt, idx, src, axis=0):
    return tgt.at[idx].add(src)

def _segment_sum(src, seg, n):
    return jax.ops.segment_sum(src, seg, n)
kernel_name = 'mk_hybrid_d2_jaxref_r8_900600'

def setup_inputs(seed: int=0):
    np.random.seed(seed)
    _w = jnp.asarray

    def _L0_attn_a_setup():
        import jax, jax.numpy as jnp
        import numpy as np
        N_IN = 128
        KSIZE = 31
        PAD_L = 30
        HEADS = 16
        key = jax.random.key(seed)
        k1, k2 = jax.random.split(key)
        B, T, C = (2, 256, N_IN)
        x = jax.random.normal(k1, (B, T, C), dtype=jnp.float32)
        w_lin = jax.random.normal(k2, (HEADS * KSIZE, C), dtype=jnp.float32) * (1.0 / np.sqrt(C))
        return {'x': x, 'w_lin': w_lin}
    _L0_attn_a_in = _L0_attn_a_setup()

    def _L0_attn_b_setup():
        import jax, jax.numpy as jnp
        import numpy as np
        _PAIRS = [(0, 1), (0, 2), (0, 3), (1, 2), (1, 3), (2, 3)]
        _J6 = jnp.array([[0, 0, 0, 0, 0, 1], [0, 0, 0, 0, -1, 0], [0, 0, 0, 1, 0, 0], [0, 0, 1, 0, 0, 0], [0, -1, 0, 0, 0, 0], [1, 0, 0, 0, 0, 0]], dtype=jnp.float32)

        def exterior(p1, p2):
            parts = [p1[..., i] * p2[..., j] - p1[..., j] * p2[..., i] for i, j in _PAIRS]
            L = jnp.stack(parts, axis=-1)
            n = jnp.maximum(jnp.linalg.norm(L, axis=-1, keepdims=True), 1e-12)
            return L / n
        key = jax.random.key(seed)
        B, T, D, H = (4, 256, 128, 16)
        ks = jax.random.split(key, 10)
        s = 0.02
        return {'x': jax.random.normal(ks[0], (B, T, D), dtype=jnp.float32), 'W1_q': jax.random.normal(ks[1], (2 * D, 4 * H), dtype=jnp.float32) * s, 'W2_q': jax.random.normal(ks[2], (2 * D, 4 * H), dtype=jnp.float32) * s, 'W1_k': jax.random.normal(ks[3], (D, 4 * H), dtype=jnp.float32) * s, 'W2_k': jax.random.normal(ks[4], (D, 4 * H), dtype=jnp.float32) * s, 'W_v': jax.random.normal(ks[5], (D, D), dtype=jnp.float32) * s, 'b_v': jnp.zeros((D,), dtype=jnp.float32), 'W_o': jax.random.normal(ks[6], (D, D), dtype=jnp.float32) * s, 'b_o': jnp.zeros((D,), dtype=jnp.float32)}
    _L0_attn_b_in = _L0_attn_b_setup()

    def _L0_ffn_setup():
        import jax, jax.numpy as jnp
        import numpy as np
        LN_EPS = 0.001
        EPS = 1e-05
        QB = 128.0

        def ste_round(x):
            return x + jax.lax.stop_gradient(jnp.round(x) - x)
        key = jax.random.key(seed)
        k1, k2 = jax.random.split(key)
        x = jax.random.normal(k1, (4, 1024, 128), dtype=jnp.float32)
        weight = jax.random.normal(k2, (128, 128), dtype=jnp.float32) * 0.02
        ln_gamma = jnp.ones((128,), dtype=jnp.float32)
        ln_beta = jnp.zeros((128,), dtype=jnp.float32)
        return {'x': x, 'weight': weight, 'ln_gamma': ln_gamma, 'ln_beta': ln_beta}
    _L0_ffn_in = _L0_ffn_setup()

    def _L1_attn_a_setup():
        import jax, jax.numpy as jnp
        import numpy as np
        B, N, D = (8, 512, 128)
        key = jax.random.key(seed)
        k1, k2 = jax.random.split(key)
        x = jax.random.normal(k1, (B, N, D), dtype=jnp.float32)
        t = jax.random.normal(k2, (N, D), dtype=jnp.float32)
        return {'x': x, 't': t}
    _L1_attn_a_in = _L1_attn_a_setup()

    def _L1_attn_b_setup():
        import jax, jax.numpy as jnp
        import numpy as np
        DIM = 128
        EXPAND = 2
        INNER = DIM * EXPAND
        B = 4
        S = 256
        EPS = 1e-06

        def _linear_params(key, fan_in, fan_out):
            kw, kb = jax.random.split(key)
            bound = 1.0 / np.sqrt(fan_in)
            w = jax.random.uniform(kw, (fan_out, fan_in), jnp.float32, -bound, bound)
            b = jax.random.uniform(kb, (fan_out,), jnp.float32, -bound, bound)
            return (w, b)
        key = jax.random.key(seed)
        ks = jax.random.split(key, 8)
        x = jax.random.normal(ks[0], (B, S, DIM), jnp.float32)
        in_w, in_b = _linear_params(ks[1], DIM, INNER)
        gate_w, gate_b = _linear_params(ks[2], DIM, INNER)
        b_w, b_b = _linear_params(ks[3], INNER, INNER)
        c_w, c_b = _linear_params(ks[4], INNER, INNER)
        d_w, d_b = _linear_params(ks[5], INNER, INNER)
        out_w, out_b = _linear_params(ks[6], INNER, DIM)
        a_log = jnp.zeros((INNER,), jnp.float32)
        norm_w = jnp.ones((DIM,), jnp.float32)
        return {'x': x, 'norm_w': norm_w, 'in_w': in_w, 'in_b': in_b, 'gate_w': gate_w, 'gate_b': gate_b, 'b_w': b_w, 'b_b': b_b, 'c_w': c_w, 'c_b': c_b, 'd_w': d_w, 'd_b': d_b, 'out_w': out_w, 'out_b': out_b, 'a_log': a_log}
    _L1_attn_b_in = _L1_attn_b_setup()

    def _L1_ffn_setup():
        import jax, jax.numpy as jnp
        import numpy as np
        DIM = 128

        def _reference_tuple_inner(x, W_r, W_k, W_v, mu_r, mu_k):
            B, T, C = x.shape
            x_prev = jnp.concatenate([jnp.zeros((B, 1, C), x.dtype), x[:, :-1, :]], axis=1)
            xr = mu_r * x + (1.0 - mu_r) * x_prev
            xk = mu_k * x + (1.0 - mu_k) * x_prev
            r = jax.nn.sigmoid(jnp.einsum('btc,dc->btd', xr, W_r))
            k = jnp.einsum('btc,dc->btd', xk, W_k)
            k_act = jnp.square(jax.nn.relu(k))
            out = r * jnp.einsum('btc,dc->btd', k_act, W_v)
            new_state = x[:, -1, :]
            return (out, new_state)
        key = jax.random.key(seed)
        ks = jax.random.split(key, 6)
        B, T, C = (8, 256, DIM)
        x = jax.random.normal(ks[0], (B, T, C), dtype=jnp.float32)
        s = 1.0 / np.sqrt(C)
        W_r = jax.random.uniform(ks[1], (C, C), jnp.float32, -s, s)
        W_k = jax.random.uniform(ks[2], (C, C), jnp.float32, -s, s)
        W_v = jax.random.uniform(ks[3], (C, C), jnp.float32, -s, s)
        mu_r = jax.random.uniform(ks[4], (C,), jnp.float32)
        mu_k = jax.random.uniform(ks[5], (C,), jnp.float32)
        return {'x': x, 'W_r': W_r, 'W_k': W_k, 'W_v': W_v, 'mu_r': mu_r, 'mu_k': mu_k}
    _L1_ffn_in = _L1_ffn_setup()
    _d = {'L0_attn_a_x': _L0_attn_a_in['x'], 'L0_attn_a_w_lin': _L0_attn_a_in['w_lin'], 'L0_attn_b_W1_q': _L0_attn_b_in['W1_q'], 'L0_attn_b_W2_q': _L0_attn_b_in['W2_q'], 'L0_attn_b_W1_k': _L0_attn_b_in['W1_k'], 'L0_attn_b_W2_k': _L0_attn_b_in['W2_k'], 'L0_attn_b_W_v': _L0_attn_b_in['W_v'], 'L0_attn_b_b_v': _L0_attn_b_in['b_v'], 'L0_attn_b_W_o': _L0_attn_b_in['W_o'], 'L0_attn_b_b_o': _L0_attn_b_in['b_o'], 'L0_ffn_weight': _L0_ffn_in['weight'], 'L0_ffn_ln_gamma': _L0_ffn_in['ln_gamma'], 'L0_ffn_ln_beta': _L0_ffn_in['ln_beta'], 'L1_attn_a_t': _L1_attn_a_in['t'], 'L1_attn_b_norm_w': _L1_attn_b_in['norm_w'], 'L1_attn_b_in_w': _L1_attn_b_in['in_w'], 'L1_attn_b_in_b': _L1_attn_b_in['in_b'], 'L1_attn_b_gate_w': _L1_attn_b_in['gate_w'], 'L1_attn_b_gate_b': _L1_attn_b_in['gate_b'], 'L1_attn_b_b_w': _L1_attn_b_in['b_w'], 'L1_attn_b_b_b': _L1_attn_b_in['b_b'], 'L1_attn_b_c_w': _L1_attn_b_in['c_w'], 'L1_attn_b_c_b': _L1_attn_b_in['c_b'], 'L1_attn_b_d_w': _L1_attn_b_in['d_w'], 'L1_attn_b_d_b': _L1_attn_b_in['d_b'], 'L1_attn_b_out_w': _L1_attn_b_in['out_w'], 'L1_attn_b_out_b': _L1_attn_b_in['out_b'], 'L1_attn_b_a_log': _L1_attn_b_in['a_log'], 'L1_ffn_W_r': _L1_ffn_in['W_r'], 'L1_ffn_W_k': _L1_ffn_in['W_k'], 'L1_ffn_W_v': _L1_ffn_in['W_v'], 'L1_ffn_mu_r': _L1_ffn_in['mu_r'], 'L1_ffn_mu_k': _L1_ffn_in['mu_k']}
    _x0 = _d['L0_attn_a_x']
    _d['L0_attn_a_x'] = jax.random.normal(jax.random.fold_in(jax.random.key(seed), 1), (8, 512, 128), dtype=_x0.dtype)
    del _x0
    return _d

def reference(L0_attn_a_x, L0_attn_a_w_lin, L0_attn_b_W1_q, L0_attn_b_W2_q, L0_attn_b_W1_k, L0_attn_b_W2_k, L0_attn_b_W_v, L0_attn_b_b_v, L0_attn_b_W_o, L0_attn_b_b_o, L0_ffn_weight, L0_ffn_ln_gamma, L0_ffn_ln_beta, L1_attn_a_t, L1_attn_b_norm_w, L1_attn_b_in_w, L1_attn_b_in_b, L1_attn_b_gate_w, L1_attn_b_gate_b, L1_attn_b_b_w, L1_attn_b_b_b, L1_attn_b_c_w, L1_attn_b_c_b, L1_attn_b_d_w, L1_attn_b_d_b, L1_attn_b_out_w, L1_attn_b_out_b, L1_attn_b_a_log, L1_ffn_W_r, L1_ffn_W_k, L1_ffn_W_v, L1_ffn_mu_r, L1_ffn_mu_k):

    def _L0_attn_a_ref(x, w_lin):
        import jax, jax.numpy as jnp
        import numpy as np
        N_IN = 128
        KSIZE = 31
        PAD_L = 30
        HEADS = 16
        B, T, C = x.shape
        H, K, P = (HEADS, KSIZE, PAD_L)
        R = C // H
        w = jnp.einsum('btc,fc->btf', x, w_lin).reshape(B, T, H, K)
        w = jax.nn.softmax(w.astype(jnp.float32), axis=-1).astype(x.dtype)
        w = w.transpose(0, 2, 1, 3)
        t_idx = jnp.arange(T)[:, None]
        s_idx = jnp.arange(T)[None, :]
        kidx = s_idx - t_idx + P
        mask = (kidx >= 0) & (kidx < K)
        kidx_c = jnp.clip(kidx, 0, K - 1)
        we = jnp.take_along_axis(w, jnp.broadcast_to(kidx_c, (B, H, T, T)), axis=-1)
        we = jnp.where(mask, we, jnp.zeros((), dtype=we.dtype))
        xh = x.reshape(B, T, H, R).transpose(0, 2, 1, 3)
        out = jnp.einsum('bhts,bhsr->bhtr', we, xh)
        return out.transpose(0, 2, 1, 3).reshape(B, T, C)

    def _L0_attn_b_ref(x, W1_q, W2_q, W1_k, W2_k, W_v, b_v, W_o, b_o):
        import jax, jax.numpy as jnp
        import numpy as np
        _PAIRS = [(0, 1), (0, 2), (0, 3), (1, 2), (1, 3), (2, 3)]
        _J6 = jnp.array([[0, 0, 0, 0, 0, 1], [0, 0, 0, 0, -1, 0], [0, 0, 0, 1, 0, 0], [0, 0, 1, 0, 0, 0], [0, -1, 0, 0, 0, 0], [1, 0, 0, 0, 0, 0]], dtype=jnp.float32)

        def exterior(p1, p2):
            parts = [p1[..., i] * p2[..., j] - p1[..., j] * p2[..., i] for i, j in _PAIRS]
            L = jnp.stack(parts, axis=-1)
            n = jnp.maximum(jnp.linalg.norm(L, axis=-1, keepdims=True), 1e-12)
            return L / n
        B, T, D = x.shape
        H = W1_k.shape[1] // 4
        d_head = D // H
        scale = 6.0 ** (-0.5)
        x_prev = jnp.concatenate([jnp.zeros((B, 1, D), dtype=x.dtype), x[:, :-1]], axis=1)
        x_bigram = jnp.concatenate([x, x_prev], axis=-1)
        q1 = (x_bigram @ W1_q).reshape(B, T, H, 4)
        q2 = (x_bigram @ W2_q).reshape(B, T, H, 4)
        L_q = exterior(q1, q2)
        k1 = (x @ W1_k).reshape(B, T, H, 4)
        k2 = (x @ W2_k).reshape(B, T, H, 4)
        L_k = exterior(k1, k2)
        JL_k = L_k @ _J6.T
        attn = jnp.einsum('bqhc,bkhc->bhqk', L_q, JL_k) * scale
        causal = jnp.tril(jnp.ones((T, T), dtype=bool))
        attn = jnp.where(causal, attn, -jnp.inf)
        attn = jax.nn.softmax(attn, axis=-1)
        v = (x @ W_v + b_v).reshape(B, T, H, d_head)
        out = jnp.einsum('bhqk,bkhd->bqhd', attn, v).reshape(B, T, D)
        return out @ W_o + b_o

    def _L0_ffn_ref(x, weight, ln_gamma, ln_beta):
        import jax, jax.numpy as jnp
        import numpy as np
        LN_EPS = 0.001
        EPS = 1e-05
        QB = 128.0

        def ste_round(x):
            return x + jax.lax.stop_gradient(jnp.round(x) - x)
        mu = jnp.mean(x, axis=-1, keepdims=True)
        var = jnp.var(x, axis=-1, keepdims=True)
        xn = (x - mu) * jax.lax.rsqrt(var + LN_EPS) * ln_gamma + ln_beta
        beta = jnp.mean(jnp.abs(weight))
        w_q = jnp.clip(ste_round(weight / (beta + EPS)), -1.0, 1.0)
        gamma = jnp.max(jnp.abs(xn))
        xq = jnp.clip(xn * QB / gamma, -QB + EPS, QB - EPS)
        y = jnp.einsum('bsd,du->bsu', xq, w_q)
        return y * (gamma * beta / QB)

    def _L1_attn_a_ref(x, t):
        import jax, jax.numpy as jnp
        import numpy as np
        B, N, D = (8, 512, 128)
        'Causal per-channel Toeplitz mix: y[b,i,d] = sum_{j<=i} t[i-j,d] * x[b,j,d].\n\n            Computed via zero-padded FFT convolution (O(n log n) per channel) instead of\n            the O(n^2) dense triangular matmul; the causal truncation [:n] keeps only the\n            lower-triangular (relative-position j<=i) contributions, matching the CUDA kernel.\n            '
        b, n, d = x.shape
        L = 2 * n
        Xf = jnp.fft.rfft(x, n=L, axis=1)
        Tf = jnp.fft.rfft(t, n=L, axis=0)
        y = jnp.fft.irfft(Xf * Tf[None], n=L, axis=1)[:, :n, :]
        return y.astype(x.dtype)

    def _L1_attn_b_ref(x, norm_w, in_w, in_b, gate_w, gate_b, b_w, b_b, c_w, c_b, d_w, d_b, out_w, out_b, a_log):
        import jax, jax.numpy as jnp
        import numpy as np
        DIM = 128
        EXPAND = 2
        INNER = DIM * EXPAND
        B = 4
        S = 256
        EPS = 1e-06

        def _linear_params(key, fan_in, fan_out):
            kw, kb = jax.random.split(key)
            bound = 1.0 / np.sqrt(fan_in)
            w = jax.random.uniform(kw, (fan_out, fan_in), jnp.float32, -bound, bound)
            b = jax.random.uniform(kb, (fan_out,), jnp.float32, -bound, bound)
            return (w, b)
        residual = x
        xn = x * jax.lax.rsqrt(jnp.mean(x * x, axis=-1, keepdims=True) + EPS) * norm_w
        u = jnp.einsum('bsd,id->bsi', xn, in_w) + in_b
        g = jax.nn.sigmoid(jnp.einsum('bsd,id->bsi', xn, gate_w) + gate_b)
        u = u * g
        b = jnp.einsum('bsi,ji->bsj', u, b_w) + b_b
        c = jnp.einsum('bsi,ji->bsj', u, c_w) + c_b
        d = jnp.einsum('bsi,ji->bsj', u, d_w) + d_b
        a = jnp.exp(-jax.nn.softplus(a_log))

        def step(h, b_t):
            h = a * h + b_t
            return (h, h)
        h0 = jnp.zeros((x.shape[0], b.shape[-1]), x.dtype)
        _, hs = jax.lax.scan(step, h0, jnp.swapaxes(b, 0, 1))
        hs = jnp.swapaxes(hs, 0, 1)
        y = c * hs + d
        y = jnp.einsum('bsi,di->bsd', y, out_w) + out_b
        return residual + y

    def _L1_ffn_ref(x, W_r, W_k, W_v, mu_r, mu_k):
        import jax, jax.numpy as jnp
        import numpy as np
        DIM = 128

        def _reference_tuple_inner(x, W_r, W_k, W_v, mu_r, mu_k):
            B, T, C = x.shape
            x_prev = jnp.concatenate([jnp.zeros((B, 1, C), x.dtype), x[:, :-1, :]], axis=1)
            xr = mu_r * x + (1.0 - mu_r) * x_prev
            xk = mu_k * x + (1.0 - mu_k) * x_prev
            r = jax.nn.sigmoid(jnp.einsum('btc,dc->btd', xr, W_r))
            k = jnp.einsum('btc,dc->btd', xk, W_k)
            k_act = jnp.square(jax.nn.relu(k))
            out = r * jnp.einsum('btc,dc->btd', k_act, W_v)
            new_state = x[:, -1, :]
            return (out, new_state)
        return _reference_tuple_inner(x, W_r, W_k, W_v, mu_r, mu_k)[0]
    x = L0_attn_a_x
    x = x + _L0_attn_a_ref(_layernorm(x, axis=-1), L0_attn_a_w_lin)
    x = x + _L0_ffn_ref(_layernorm(x, axis=-1), L0_ffn_weight, L0_ffn_ln_gamma, L0_ffn_ln_beta)
    x = x + _L0_attn_b_ref(_layernorm(x, axis=-1), L0_attn_b_W1_q, L0_attn_b_W2_q, L0_attn_b_W1_k, L0_attn_b_W2_k, L0_attn_b_W_v, L0_attn_b_b_v, L0_attn_b_W_o, L0_attn_b_b_o)
    x = x + _L0_ffn_ref(_layernorm(x, axis=-1), L0_ffn_weight, L0_ffn_ln_gamma, L0_ffn_ln_beta)
    x = x + _L1_attn_a_ref(_layernorm(x, axis=-1), L1_attn_a_t)
    x = x + _L1_ffn_ref(_layernorm(x, axis=-1), L1_ffn_W_r, L1_ffn_W_k, L1_ffn_W_v, L1_ffn_mu_r, L1_ffn_mu_k)
    x = x + _L1_attn_b_ref(_layernorm(x, axis=-1), L1_attn_b_norm_w, L1_attn_b_in_w, L1_attn_b_in_b, L1_attn_b_gate_w, L1_attn_b_gate_b, L1_attn_b_b_w, L1_attn_b_b_b, L1_attn_b_c_w, L1_attn_b_c_b, L1_attn_b_d_w, L1_attn_b_d_b, L1_attn_b_out_w, L1_attn_b_out_b, L1_attn_b_a_log)
    x = x + _L1_ffn_ref(_layernorm(x, axis=-1), L1_ffn_W_r, L1_ffn_W_k, L1_ffn_W_v, L1_ffn_mu_r, L1_ffn_mu_k)
    return x

_drawn_inputs = setup_inputs


def setup_inputs(seed=0):
    import zlib

    import numpy as np

    out = dict(_drawn_inputs(seed))
    spreads = {'L0_attn_b_b_v': (0.0, 0.436),
     'L0_attn_b_b_o': (0.0, 0.1),
     'L0_ffn_ln_gamma': (1.0, 0.2),
     'L0_ffn_ln_beta': (0.0, 0.294),
     'L1_attn_b_norm_w': (1.0, 0.6),
     'L1_attn_b_a_log': (0.0, 0.8)}
    factors = {'L0_attn_b_W1_q': 8.0,
     'L0_attn_b_W2_q': 8.0,
     'L0_attn_b_W1_k': 8.0,
     'L0_attn_b_W2_k': 8.0,
     'L0_attn_b_W_v': 6.572,
     'L1_attn_b_in_w': 8.0,
     'L1_attn_b_in_b': 8.0,
     'L1_attn_b_gate_w': 8.0,
     'L1_attn_b_gate_b': 8.0,
     'L1_attn_b_b_w': 8.0,
     'L1_attn_b_b_b': 8.0,
     'L1_attn_b_c_w': 8.0,
     'L1_attn_b_c_b': 39.126,
     'L1_attn_b_d_w': 8.0,
     'L1_attn_b_d_b': 64.0,
     'L1_attn_b_out_w': 8.0,
     'L1_attn_b_out_b': 64.0,
     'L1_ffn_W_r': 8.0,
     'L1_ffn_W_k': 6.236,
     'L1_ffn_W_v': 5.784,
     'L1_ffn_mu_r': 8.0,
     'L1_ffn_mu_k': 8.0}
    for name, (base, spread) in spreads.items():
        noise = np.random.default_rng([zlib.crc32(name.encode()), seed]).standard_normal(out[name].shape)
        drawn = base * np.exp(spread * noise) if base else spread * noise
        out[name] = jnp.asarray(drawn.astype(out[name].dtype))
    for name, factor in factors.items():
        out[name] = (out[name] * factor).astype(out[name].dtype)
    return out
```

```python
from contextlib import ExitStack

import numpy as np
import concourse.bass as bass
from concourse import mybir

ALU = mybir.AluOpType
ACT = mybir.ActivationFunctionType
AX = mybir.AxisListType
F32 = mybir.dt.float32
BF16 = mybir.dt.bfloat16

P = 128
B, T, C = 8, 512, 128
NT = T // P
HEADS, TAPS = 16, 31
REACH = TAPS - 1
R = C // HEADS
OWN = B * T // P
PER_SEQ = T // OWN
POOL_TAPS = 11
PAIRS6 = [(0, 1), (0, 2), (0, 3), (1, 2), (1, 3), (2, 3)]
D_HEAD = C // HEADS
PAIRS = HEADS // 2
KB = 64
NJ = T // KB
COMPS = 6
SLOTS = 6
ROWS_B = 64
QK_ROWS = ROWS_B + SLOTS * COMPS
SCALE = float(COMPS) ** -0.5
UNITS = 18
CHUNKS = 6
CHUNK_BLOCKS = ([(0, 0), (1, 512), (7, 960)], [(2, 0), (6, 384), (3, 512), (5, 832)], [(4, 0)])
D_FFN_EPS = 1e-3
LN_EPS = 1e-5
NORM_EPS = 1e-6
QUANT = 128.0
CLIP = float(np.float32(QUANT - 1e-5)) / QUANT
WIN = 256
INNER = 256
SHARED = 36600
MI = INNER // P
STAGES = ("conv", "ffn0", "attn", "ffn1", "toep", "mix0", "scan", "mix1")


def program(nc, d, out, stages=STAGES):
    ctx = ExitStack()
    with ctx:
        def sb(name, shape, dt=F32):
            return ctx.enter_context(nc.sbuf_tensor(name, shape, dt))

        def sem(name):
            return ctx.enter_context(nc.semaphore(name))

        ps = ctx.enter_context(nc.psum_tensor("ps", [P, 8 * 512], F32))

        def bank(i, n=1):
            return ps[:, 512 * i:512 * (i + n)]

        shared = sb("shared", [P, SHARED])
        cursor = [0]

        def part(shape, dt=F32):
            size = int(np.prod(shape)) * (4 if dt == F32 else 2) // 4
            a = cursor[0]
            cursor[0] += size
            assert cursor[0] <= SHARED
            v = shared[:, a:a + size]
            if dt != F32:
                v = v.bitcast(dt)
            names = "abcd"[:len(shape)]
            if len(shape) > 1:
                v = v.rearrange(f"p ({' '.join(names)}) -> p {' '.join(names)}", **dict(zip(names, shape)))
            return v

        x_tile = sb("x_tile", [P, B * NT * C])
        x_blk = part([OWN * C])
        y_ext = part([(REACH + OWN) * C])
        prod = [part([TAPS * C]) for q in range(2)]
        ident = sb("ident", [P, P])
        ident_b = sb("ident_b", [P, P], BF16)
        minus_half = sb("minus_half", [P, OWN])
        w_conv = part([TAPS * HEADS])
        st_c = part([OWN, 6])
        mv_c = part([OWN, 2])
        arg_c = part([OWN])
        rstd_c = part([OWN])
        y_cur = [part([C]) for q in range(2)]
        yT_cur = [part([P]) for q in range(2)]
        mx = [part([HEADS]) for q in range(2)]
        logit = [part([TAPS * HEADS]) for q in range(2)]
        e_w = [part([TAPS * HEADS]) for q in range(2)]
        esum = [part([HEADS]) for q in range(2)]
        erec = [part([HEADS]) for q in range(2)]
        avg = [part([C]) for q in range(2)]

        st = [sb(f"st{q}", [P, NT, 6]) for q in range(2)]
        mv = [sb(f"mv{q}", [P, NT, 2]) for q in range(2)]
        arg = [sb(f"arg{q}", [P, 3, NT]) for q in range(2)]
        expo = sb("expo", [P, 3, NT])
        rstd = [sb(f"rstd{q}", [P, 3, NT]) for q in range(2)]
        z = [sb(f"z{q}", [P, NT, C]) for q in range(2)]

        cursor[0] = 0
        xnT = part([B * T])
        gam_beta = sb("gam_beta", [P, 2])
        w_q = sb("w_q", [P, C])
        w_raw = sb("w_raw", [P, C])
        w_scr = sb("w_scr", [P, C])
        w_beta = sb("w_beta", [P, 4])
        ones = sb("ones", [P, P])
        amax = sb("amax", [P, B])
        amax1 = sb("amax1", [P, 1])
        gmax = sb("gmax", [P, 1])
        bound = sb("bound", [P, 2])
        clipped = [part([T]) for q in range(2)]

        dft_f = sb("dft_f", [P, 2, 6 * P])
        dft_i = sb("dft_i", [P, 4, WIN])
        sgn = sb("sgn", [P, 1])
        t_in = sb("t_in", [P, NT, C])
        kf = [sb(f"kf{j}", [P, 3, 2, C]) for j in range(2)]
        xi_sb = None
        cursor[0] = 0
        qT = [part([PAIRS, T], BF16) for q in range(2)]
        kT = [part([PAIRS, NJ, 2 * KB], BF16) for q in range(2)]
        split_q = part([NT * HEADS, ROWS_B], BF16)
        split_k = part([NT * HEADS, ROWS_B], BF16)
        coord = part([2, 2 * NT * HEADS, 6])
        m_a = part([2, NT * HEADS, COMPS])
        m_b = part([2, NT * HEADS, COMPS])
        line = part([2, NT * HEADS, COMPS])
        rest = part([2, NT * HEADS, COMPS])
        len2 = part([2 * NT * HEADS])
        inv_len = part([2 * NT * HEADS])
        half_len = part([2 * NT * HEADS])
        v_pair = [part([NJ, PAIRS, 32]) for q in range(2)]
        probs = [part([4, 1024]) for q in range(2)]
        probs_c2 = part([4, 256])
        pv_sb = part([T])
        inv_den = part([NT, 8])
        att = part([NT, C])
        attT = part([T])
        w_qk = sb("w_qk", [P, 2, C])
        w_qp = sb("w_qp", [P, 2, C // 2])
        w_val = sb("w_val", [P, C])
        w_o = sb("w_o", [P, C])
        b_v = sb("b_v", [P, 1])
        b_v_wide = sb("b_v_wide", [P, P])
        ones_row = sb("ones_row", [1, P])
        b_o_row = sb("b_o_row", [1, C])
        att_bias = sb("att_bias", [P, C])
        mask = sb("mask", [P, KB])

        cursor[0] = 0
        pr = [part([2, 2, C]) for n in range(4)]
        pu = [part([2, C]) for n in range(4)]
        yf = [part([2, 2, 2, C]) for q in range(2)]

        w_r = sb("w_r", [P, C])
        w_k = sb("w_k", [P, C])
        w_v = sb("w_v", [P, C])
        mus = sb("mus", [P, 2])
        zT = [sb(f"zT{q}", [P, 1 + T]) for q in range(2)]
        cursor[0] = 0
        dif = [part([T]) for q in range(2)]
        xrT = [part([T]) for q in range(2)]
        xkT = [part([T]) for q in range(2)]
        kact = [part([T]) for q in range(2)]
        rsig = [part([NT * C]) for q in range(2)]
        gated = [part([NT * C]) for q in range(2)]

        w_in = sb("w_in", [P, INNER])
        w_gate = sb("w_gate", [P, INNER])
        w_b = sb("w_b", [P, MI, INNER])
        w_c = sb("w_c", [P, MI, INNER])
        w_d = sb("w_d", [P, MI, INNER])
        w_out = sb("w_out", [P, MI, C])
        w_od = sb("w_od", [P, MI, C])
        vecs = sb("vecs", [P, 6, MI])
        norm_w = sb("norm_w", [P, 1])
        decay = sb("decay", [P, MI])
        decay_row = part([MI, T])
        out_b_row = sb("out_b_row", [1, C])
        bias_row = sb("bias_row", [P, C])
        x_plus = [part([NT * C]) for q in range(2)]
        gate = [part([T]) for m in range(MI)]
        uT = [part([MI, T]) for q in range(2)]
        bT = [part([T]) for m in range(MI)]
        hT = [part([T]) for m in range(MI)]
        chT = [part([MI, T]) for q in range(2)]
        x_dram = nc.dram_tensor("x_after_conv", (B * T, C), F32).ap()

        S = {}

        def s(name):
            if name not in S:
                S[name] = sem(name)
            return S[name]

        CARRY = {}
        COLUMNS = []

        def at(e, name, count):
            e.wait_ge(s(name), count)
            if not isinstance(count, int):
                if id(e) not in CARRY:
                    CARRY[id(e)] = e.alloc_register(f"carry{len(CARRY)}")
                if e is nc.scalar:
                    e.reg_mov(CARRY[id(e)], 0)
                else:
                    e.reg_alu(CARRY[id(e)], count, 1, ALU.add)

        def column(e, value, most):
            if isinstance(value, int):
                return value
            reg = e.alloc_register(f"column{len(COLUMNS)}")
            COLUMNS.append(reg)
            e.reg_mov(reg, value)
            return e.snap(reg, min_val=0, max_val=most)

        def pairs(e, body, ahead=False, behind=False, count=B):
            if behind:
                body(0, 0)
                body(1, 1)
            with e.Fori(2 if behind else 0, (count - 2 if ahead else count) - 1, 2) as b:
                body(b, 0)
                body(b + 1, 1)
            if ahead:
                body(count - 2, 0)
                body(count - 1, 1)

        def tok(b, n=NT):
            if isinstance(b, int):
                return slice(b * T, b * T + T)
            return bass.ds(b * T, T)

        def tile(b, i):
            if isinstance(b, int):
                return slice((b * NT + i) * C, (b * NT + i + 1) * C)
            return bass.ds(b * T + i * C, C)

        def vtok(b, k):
            return slice(k, k + 1)

        ln_stages = [x for x in STAGES if x != "conv" and x in stages]
        turn_stages = [x for x in ln_stages if x != "toep"]
        upd = {x: n for n, x in enumerate(ln_stages)}
        turn = {x: n for n, x in enumerate(turn_stages)}

        def ln_stats(e, stage, b, q, fac, add, extra=False):
            n = B * upd[stage] + b
            if upd[stage] == 0:
                at(e, "x_loaded", 16 * b + 16)
            else:
                at(e, "x_updated", n - B + B * 0 + 1)
            for i in range(NT):
                e.bn_stats(st[q][:, i, :], x_tile[:, tile(b, i)])
            e.drain()
            for i in range(NT):
                e.bn_aggr(mv[q][:, i, :], st[q][:, i, :])
            e.drain()
            ins = e.tensor_scalar(arg[q][:, 0, :], mv[q][:, :, 1], fac, add, ALU.mult, ALU.add)
            if extra:
                e.tensor_scalar(arg[q][:, 1, :], mv[q][:, :, 1], fac, add, ALU.mult, ALU.add)
                ins = e.tensor_scalar(arg[q][:, 2, :], mv[q][:, :, 1], LN_EPS, None, ALU.add)
            ins.then_inc(s("var_ready"), 1)

        def ln_rstd(e, stage, b, q, k=1):
            n = B * upd[stage] + b
            e.wait_ge(s("var_ready"), n + 1)
            e.tensor_tensor(rstd[q][:, 0:k, :], arg[q][:, 0:k, :], expo[:, 0:k, :], ALU.pow).then_inc(s("rstd_ready"), 1)

        def ln_norm(e, stage, b, q):
            n = B * upd[stage] + b
            e.wait_ge(s("rstd_ready"), n + 1)
            if not (isinstance(b, int) and b < 2):
                if stage == "toep":
                    at(e, "toep_z_used", b - 1)
                else:
                    at(e, "turned", B * turn[stage] + b - 1)
            for i in range(NT):
                ins = e.tensor_scalar(z[q][:, i, :], x_tile[:, tile(b, i)], mv[q][:, i, 0:1], rstd[q][:, 0, i:i + 1],
                                      ALU.subtract, ALU.mult)
            ins.then_inc(s("z_ready"), 1)

        def turn_z(e, stage, b, q):
            e.wait_ge(s("z_ready"), B * upd[stage] + b + 1)
            e.wait_ge(s("turn_bank_free"), B * turn[stage] + b + 1)
            for i in range(NT):
                ins = e.transpose(bank(6 + q)[:, P * i:P * i + P], z[q][:, i, :], ident[:, :])
            ins.then_inc(s("turned"), 1)

        LN_CONST = {"ffn": (1 + D_FFN_EPS, LN_EPS * D_FFN_EPS), "plain": (1.0, LN_EPS),
                    "scan": (1 + NORM_EPS, LN_EPS * NORM_EPS)}
        kind = {"ffn0": "ffn", "ffn1": "ffn", "attn": "plain", "toep": "plain", "mix0": "plain", "mix1": "plain",
                "scan": "scan"}
        N_LOAD = 30
        block = ctx.enter_context(nc.Block())

        def stage_gate(e, stage):
            if upd[stage] > 0:
                e.wait_ge(s("x_updated"), B * upd[stage])

        @block.sync
        def _(e):
            e.dma_start(x_blk[:, 0:OWN * C // 2], d["x"][:, 0:OWN * C // 2]).then_inc(s("x_blk_lo"), 16)
            e.dma_start(x_blk[:, OWN * C // 2:], d["x"][:, OWN * C // 2:]).then_inc(s("x_blk_hi"), 16)
            loads = [(ident[:, :], d["ident"]), (w_conv[:, :], d["w_lin"]), (gam_beta[:, :], d["gam_beta"]),
                     (w_raw[:, :], d["weight"]), (dft_f[:, :, :], d["dft_f"]), (dft_i[:, :, :], d["dft_i"]),
                     (sgn[:, :], d["sgn"]), (t_in[:, :, :], d["t"]), (w_r[:, :], d["W_r"]), (w_k[:, :], d["W_k"]),
                     (w_v[:, :], d["W_v"]), (mus[:, :], d["mus"]), (w_in[:, :], d["in_w"]), (w_gate[:, :], d["gate_w"]),
                     (w_b[:, :, :], d["b_w"]), (w_c[:, :, :], d["c_w"]), (w_d[:, :, :], d["d_w"]),
                     (w_out[:, :, :], d["out_w"]), (vecs[:, :, :], d["vecs"]), (norm_w[:, :], d["norm_w"]),
                     (out_b_row[:, :], d["out_b"]), (expo[:, :, :], d["expo"]), (minus_half[:, :], d["minus_half"]),
                     (w_qk[:, :, :], d["w_qk"]), (w_qp[:, :, :], d["w_qp"]), (w_val[:, :], d["w_val"]), (w_o[:, :], d["W_o"]),
                     (b_v[:, :], d["b_v"]), (b_o_row[:, :], d["b_o"]), (mask[:, :], d["mask"])]
            assert len(loads) == N_LOAD
            for dst, src in loads:
                e.dma_start(dst, src).then_inc(s("weights"), 16)
            if "conv" in stages:
                e.wait_ge(s("conv_y"), 1)
                e.wait_ge(s("halo_zero"), 1)
                for b in range(B):
                    lo = b * PER_SEQ
                    e.dma_start(y_ext[lo + 1:lo + PER_SEQ, 0:REACH * C],
                                y_ext[lo:lo + PER_SEQ - 1, OWN * C:(OWN + REACH) * C]).then_inc(s("halo"), 16)
                xd = x_dram.rearrange("(p t) c -> p (t c)", t=OWN)
                for n in range(0, OWN, OWN // 8):
                    cols = slice((OWN - n - OWN // 8) * C, (OWN - n) * C)
                    e.wait_ge(s("conv_x"), n + OWN // 8)
                    e.dma_start(xd[:, cols], x_blk[:, cols]).then_inc(s("x_stored"), 16)
                e.wait_ge(s("x_stored"), 16 * 8)
            src = (x_dram if "conv" in stages else d["x"].rearrange("p (t c) -> (p t) c", c=C))
            src = src.rearrange("(n p) c -> p n c", p=P)
            for b in range(B):
                e.dma_start(x_tile[:, b * T:(b + 1) * T].rearrange("p (n c) -> p n c", c=C),
                            src[:, b * NT:(b + 1) * NT, :]).then_inc(s("x_loaded"), 16)
                e.wait_ge(s("x_loaded"), 16 * b + 16)
            od = out.rearrange("(n p) c -> p n c", p=P)
            for b in range(B):
                if ln_stages:
                    e.wait_ge(s("x_updated"), B * (len(ln_stages) - 1) + b + 1)
                e.dma_start(od[:, b * NT:(b + 1) * NT, :],
                            x_tile[:, b * T:(b + 1) * T].rearrange("p (n c) -> p n c", c=C)).then_inc(s("out_stored"), 16)
            e.wait_ge(s("out_stored"), 16 * B)

        def own(n, buf_off=0):
            return bass.ds((OWN - 1) * C - n * C + buf_off, C)

        def window(n, k0, k1):
            return bass.ds((OWN - 1 + k0) * C - n * C, (k1 - k0) * C)

        @block.gpsimd
        def _(e):
            e.memset(ones[:, :], 1.0 / (P * C)).then_inc(s("ones"), 1)
            for q in range(2):
                e.memset(zT[q][:, 0:1], 0.0).then_inc(s("zT_zero"), 1)
            if "conv" in stages:
                e.memset(y_ext[:, 0:REACH * C], 0.0).then_inc(s("halo_zero"), 1)
                e.wait_ge(s("weights"), 16 * N_LOAD)
                e.wait_ge(s("conv_var"), 1)
                e.tensor_tensor(rstd_c[:, :], arg_c[:, :], minus_half[:, :], ALU.pow).then_inc(s("conv_rstd"), 1)
                e.wait_ge(s("conv_y"), 1)
                e.wait_ge(s("halo"), 16 * B)

                def taps(n, q):
                    k0 = TAPS - POOL_TAPS
                    first = column(e, (OWN - 1 + k0) * C - n * C, (OWN - 1 + k0) * C)
                    e.wait_ge(s("conv_e"), n + 1)
                    at(e, "prod_free", n + 1)
                    e.tensor_tensor(prod[q][:, k0 * C:].rearrange("p (k h r) -> p k h r", h=HEADS, r=R),
                                    y_ext[:, bass.ds(first, POOL_TAPS * C)].rearrange("p (k h r) -> p k h r", h=HEADS, r=R),
                                    e_w[q][:, k0 * HEADS:].rearrange("p (k h) -> p k h", h=HEADS).unsqueeze(3)
                                    .to_broadcast([P, POOL_TAPS, HEADS, R]), ALU.mult).then_inc(s("prod_pool"), 1)

                def add_x(n, q):
                    first = column(e, (OWN - 1) * C - n * C, (OWN - 1) * C)
                    at(e, "conv_avg", n + 1)
                    e.tensor_tensor(x_blk[:, bass.ds(first, C)], x_blk[:, bass.ds(first, C)], avg[q][:, :], ALU.add).then_inc(s("conv_x"), 1)

                taps(0, 0)
                with e.Fori(0, OWN - 3, 2) as n:
                    taps(n + 1, 1)
                    add_x(n, 0)
                    taps(n + 2, 0)
                    add_x(n + 1, 1)
                taps(OWN - 1, 1)
                add_x(OWN - 2, 0)
                add_x(OWN - 1, 1)
            else:
                e.wait_ge(s("weights"), 16 * N_LOAD)

            for stage in ln_stages:
                k = 3 if stage == "scan" else 1
                if stage == "ffn0" or stage == "ffn1":
                    pairs(e, lambda b, q: ln_rstd(e, stage, b, q))
                    e.wait_ge(s("amax"), 1 if stage == "ffn0" else 2)
                    e.partition_all_reduce(gmax[:, :], amax1[:, :], P, bass.bass_isa.ReduceOp.max).then_inc(s("gmax"), 1)
                elif stage == "attn":
                    stage_gate(e, stage)
                    for q in range(2):
                        e.memset(kT[q][:, :, :, :], 0.0)
                        e.memset(v_pair[q][:, :, :, :], 0.0)
                    e.memset(split_q[:, :, :], 0.0)
                    e.memset(split_k[:, :, :], 0.0)
                    e.memset(half_len[:, :], -0.5)
                    e.memset(ones_row[:, :], 1.0)
                    e.drain()
                    for q in range(2):
                        e.memset(v_pair[q][0:KB, :, :, D_HEAD:D_HEAD + 1], 1.0)
                        ins = e.memset(v_pair[q][KB:P, :, :, 16 + D_HEAD:17 + D_HEAD], 1.0)
                    e.drain().then_inc(s("attn_init"), 1)
                    e.wait_ge(s("att_bias"), 1)

                    def lengths(b, q):
                        e.wait_ge(s("len2"), b + 1)
                        e.tensor_tensor(inv_len[:, :], len2[:, :], half_len[:, :], ALU.pow).then_inc(s("inv_len"), 1)

                    def add_bias(b, q):
                        first = column(e, b * T, (B - 1) * T)
                        at(e, "z_ready", B * upd[stage] + b + 1)
                        xv = x_tile[:, bass.ds(first, T)] if not isinstance(first, int) else x_tile[:, first:first + T]
                        xv = xv.rearrange("p (i c) -> p i c", c=C)
                        e.tensor_tensor(xv, xv, att_bias[:, :].unsqueeze(1).to_broadcast([P, NT, C]), ALU.add).then_inc(s("x_biased"), 1)

                    def masks(b, k):
                        c = k % 3
                        e.wait_ge(s("p_ready"), UNITS * b + 9 * (k // 3) + (4, 8, 9)[c])
                        for j, col in CHUNK_BLOCKS[c]:
                            pv = probs_c2[:, :, 0:KB] if c == 2 else probs[c][:, :, col:col + KB]
                            ins = e.tensor_tensor(pv, pv, mask[:, :].unsqueeze(1).to_broadcast([P, 4, KB]), ALU.mult)
                        ins.then_inc(s("masked"), 1)

                    ln_rstd(e, stage, 0, 0)
                    lengths(0, 0)
                    add_bias(0, 0)
                    ln_rstd(e, stage, 1, 1)

                    def body(b, q):
                        last = isinstance(b, int) and b == B - 1
                        if not last:
                            add_bias(b + 1, 1 - q)
                        masks(b, 0)
                        if not last:
                            lengths(b + 1, 1 - q)
                        if not (isinstance(b, int) and b >= B - 2):
                            ln_rstd(e, stage, b + 2, q)
                        for k in range(1, CHUNKS):
                            masks(b, k)
                    pairs(e, body, ahead=True)
                elif stage == "toep":
                    def body(b, q):
                        ln_rstd(e, stage, b, q)
                        e.wait_ge(s("toep_pu"), b + 1)
                        e.tensor_tensor(pu[0][:, :, :], pu[0][:, :, :], pu[1][:, :, :], ALU.subtract)
                        e.tensor_tensor(pu[2][:, :, :], pu[2][:, :, :], pu[3][:, :, :], ALU.add).then_inc(s("toep_cross"), 1)
                    pairs(e, body)
                elif stage in ("mix0", "mix1"):
                    mb = 0 if stage == "mix0" else B

                    def body(b, q, last=False):
                        at(e, "mix_gated", mb + b + 1)
                        e.tensor_tensor(x_tile[:, tok(b)], x_tile[:, tok(b)], gated[q][:, :], ALU.add).then_inc(s("x_updated"), 1)

                    ln_rstd(e, stage, 0, 0)

                    def both(b, q):
                        if not (isinstance(b, int) and b == B - 1):
                            ln_rstd(e, stage, b + 1, 1 - q)
                        body(b, q)
                    pairs(e, both, ahead=True)
                elif stage == "scan":
                    ln_rstd(e, stage, 0, 0, 3)

                    def body(b, q):
                        e.wait_ge(s("rstd_ready"), B * upd[stage] + b + 1)
                        e.tensor_tensor(rstd[q][:, 1, :], rstd[q][:, 1, :], rstd[q][:, 2, :], ALU.mult).then_inc(s("ratio"), 1)
                        if not (isinstance(b, int) and b == B - 1):
                            ln_rstd(e, stage, b + 1, 1 - q, 3)
                    pairs(e, body, ahead=True)
                else:
                    pairs(e, lambda b, q: ln_rstd(e, stage, b, q))

        @block.tensor
        def _(e):
            e.wait_ge(s("weights"), 16 * N_LOAD)
            if "conv" in stages:
                def logits(n, q):
                    e.wait_ge(s("y_cur"), n + 1)
                    e.transpose(bank(q)[:, 0:P], y_cur[q][:, :], ident[:, :]).then_inc(s("yT_bank"), 1)
                    e.wait_ge(s("yT_cur"), n + 1)
                    if not (isinstance(n, int) and n < 2):
                        e.wait_ge(s("conv_sub"), n - 1)
                    e.matmul(bank(2 + q)[:, 0:TAPS * HEADS], yT_cur[q][:, :], w_conv[:, :], start=True, stop=True) \
                        .then_inc(s("logits"), 1)

                def total(n, q):
                    if not (isinstance(n, int) and n < 2):
                        e.wait_ge(s("conv_avg"), n - 1)
                    e.wait_ge(s("prod_vec"), n + 1)
                    for k in range(TAPS):
                        if k == TAPS - POOL_TAPS:
                            e.wait_ge(s("prod_pool"), n + 1)
                        ins = e.matmul(bank(4 + q)[:, 0:C], ident[:, :], prod[q][:, k * C:k * C + C], start=(k == 0),
                                       stop=(k == TAPS - 1))
                    ins.then_inc(s("prod_free"), 1)
                logits(0, 0)

                def body(n, q):
                    if not (isinstance(n, int) and n == OWN - 1):
                        logits(n + 1, 1 - q)
                    total(n, q)
                pairs(e, body, ahead=True, behind=True, count=OWN)

            if "ffn0" in stages:
                e.wait_ge(s("w_abs"), 1)
                e.wait_ge(s("ones"), 1)
                e.matmul(bank(5)[:, 0:1], ones[:, :], w_beta[:, 0:1], start=True, stop=True).then_inc(s("w_mean"), 1)

            for stage in ln_stages:
                if stage in ("ffn0", "ffn1"):
                    fb = 0 if stage == "ffn0" else B
                    stage_gate(e, stage)
                    pairs(e, lambda b, q: turn_z(e, stage, b, q))

                    def body(b, q):
                        e.wait_ge(s("clipped"), fb + b + 1)
                        for i in range(NT):
                            ins = e.matmul(bank(q)[:, C * i:C * i + C], clipped[q][:, P * i:P * i + P], w_q[:, :],
                                           start=True, stop=True)
                        ins.then_inc(s("ffn_y"), 1)
                    pairs(e, body)
                elif stage == "attn":
                    stage_gate(e, stage)
                    e.wait_ge(s("attn_init"), 1)
                    e.wait_ge(s("b_v_wide"), 1)
                    e.matmul(bank(4)[:, 0:C], b_v_wide[:, :], w_o[:, :], start=True, stop=False)
                    e.matmul(bank(4)[:, 0:C], ones_row[:, :], b_o_row[:, :], start=False, stop=True).then_inc(s("bias_bank"), 1)
                    nt = B * turn[stage]

                    def turn5(b, q):
                        e.wait_ge(s("z_ready"), B * upd[stage] + b + 1)
                        if not (isinstance(b, int) and b == 0):
                            e.wait_ge(s("aT_copied"), b - 1) if not (isinstance(b, int) and b == 1) else None
                        for i in range(NT):
                            ins = e.transpose(bank(5)[:, P * i:P * i + P], z[q][:, i, :], ident[:, :])
                        ins.then_inc(s("turned"), 1)

                    def project(b, q, v):
                        if v == 0:
                            e.wait_ge(s("turn_bank_free"), nt + b + 3)
                        for i in range(NT):
                            dst = bank(5 + v)[:, C * i:C * i + C]
                            e.matmul(dst, zT[q][:, 1 + P * i:1 + P * i + P], w_qk[:, v, :], start=True, stop=False)
                            ins = e.matmul(dst[:, 0:C // 2], zT[q][:, P * i:P * i + P], w_qp[:, v, :], start=False, stop=True)
                        ins.then_inc(s("coord_bank"), 1)

                    def value_rows(b, q):
                        e.wait_ge(s("coord_copied"), 2 * b + 1)
                        for j in range(NJ):
                            toks = zT[q][:, 1 + KB * j:1 + KB * j + KB]
                            e.matmul(bank(5)[0:KB, KB * j:KB * j + KB], toks, w_val[:, 0:KB], start=True, stop=True)
                            ins = e.matmul(bank(5)[KB:P, KB * j:KB * j + KB], toks, w_val[:, KB:2 * KB], start=True, stop=True)
                        ins.then_inc(s("v_bank"), 1)

                    def turn_qk(b, q, r):
                        src = split_q if r % 2 == 0 else split_k
                        p0 = 2 * (r // 2)
                        e.wait_ge(s("split"), 2 * b + 1 + r % 2)
                        if not (isinstance(b, int) and b == 0 and r == 0):
                            e.wait_ge(s("qk_copied"), 8 * b + r)
                        dst = bank(7).bitcast(BF16)
                        for p in range(2):
                            for i in range(NT):
                                rows = src[:, HEADS * i + 2 * (p0 + p):HEADS * i + 2 * (p0 + p) + 2, :].rearrange("p h r -> p (h r)")
                                ins = e.transpose(dst[0:QK_ROWS, T * p + P * i:T * p + P * i + P], rows[:, 0:QK_ROWS], ident_b[:, :])
                        ins.then_inc(s("qk_turned"), 1)

                    def scores(b, q, u):
                        g, c, i0 = u // 9, min(u % 9 // 4, 2), u % 9 % 4
                        if u == 0:
                            e.wait_ge(s("qk_copied"), 8 * b + 8)
                        if not (isinstance(b, int) and b == 0 and u < 2):
                            e.wait_ge(s("p_ready"), UNITS * b + u - 1)
                        for i in (range(4) if c == 2 else (i0,)):
                            p = 4 * g + i
                            for j, col in CHUNK_BLOCKS[c]:
                                col += 256 * i if c == 2 else 0
                                ins = e.matmul(bank(2 * (u % 2), 2)[:, col:col + T - KB * j], kT[q][0:QK_ROWS, p, j, :],
                                               qT[q][0:QK_ROWS, p, KB * j:T], start=True, stop=True)
                        ins.then_inc(s("scored"), 1)

                    def weigh(b, q, k):
                        g, c = k // 3, k % 3
                        e.wait_ge(s("masked"), CHUNKS * b + k + 1)
                        if k == 0:
                            e.wait_ge(s("v_copied"), 2 * b + 2)
                        if c == 0 and not (isinstance(b, int) and b == 0 and g == 0):
                            e.wait_ge(s("pv_copied"), 2 * b + g)
                        for j, col in CHUNK_BLOCKS[c]:
                            for i in range(4):
                                pr_ = probs_c2[:, i, :] if c == 2 else probs[c][:, i, col:col + T - KB * j]
                                ins = e.matmul(bank(4)[32 * i:32 * i + 32, KB * j:T], v_pair[q][:, j, 4 * g + i, :], pr_,
                                               start=(j == 0), stop=(j == 4))
                        ins.then_inc(s("weighed"), 1)

                    def turn_pv(b, g):
                        e.wait_ge(s("pv_copied"), 2 * b + g + 1)
                        for i in range(NT):
                            ins = e.transpose(bank(6)[:, P * i:P * i + P], pv_sb[:, P * i:P * i + P], ident[:, :])
                        ins.then_inc(s("pv_turned"), 1)

                    def turn_att(b):
                        e.wait_ge(s("att_ready"), 2 * b + 2)
                        for i in range(NT):
                            ins = e.transpose(bank(5)[:, P * i:P * i + P], att[:, i, :], ident[:, :])
                        ins.then_inc(s("att_turned"), 1)

                    def out_rows(b):
                        e.wait_ge(s("aT_copied"), b + 1)
                        for i in range(NT):
                            ins = e.matmul(bank(6)[:, C * i:C * i + C], attT[:, P * i:P * i + P], w_o[:, :], start=True, stop=True)
                        ins.then_inc(s("att_out"), 1)

                    turn5(0, 0)
                    project(0, 0, 0)
                    project(0, 0, 1)
                    value_rows(0, 0)
                    for r in range(8):
                        turn_qk(0, 0, r)

                    def body(b, q):
                        first, last = (isinstance(b, int) and b == x for x in (0, B - 1))
                        scores(b, q, 0)
                        if not first:
                            weigh(b - 1, 1 - q, 4)
                        scores(b, q, 1)
                        if not first:
                            weigh(b - 1, 1 - q, 5)
                        scores(b, q, 2)
                        if not first:
                            turn_pv(b - 1, 1)
                        scores(b, q, 3)
                        if not first:
                            turn_att(b - 1)
                        scores(b, q, 4)
                        weigh(b, q, 0)
                        scores(b, q, 5)
                        if not first:
                            out_rows(b - 1)
                        if not last:
                            e.wait_ge(s("v_copied"), 2 * b + 2)
                            turn5(b + 1, 1 - q)
                        scores(b, q, 6)
                        if not last:
                            if not first:
                                e.wait_ge(s("x_updated"), B * upd[stage] + b)
                            project(b + 1, 1 - q, 0)
                        scores(b, q, 7)
                        if not last:
                            project(b + 1, 1 - q, 1)
                        scores(b, q, 8)
                        weigh(b, q, 1)
                        scores(b, q, 9)
                        if not last:
                            value_rows(b + 1, 1 - q)
                        scores(b, q, 10)
                        weigh(b, q, 2)
                        scores(b, q, 11)
                        scores(b, q, 12)
                        if not last:
                            e.wait_ge(s("coord_copied"), 2 * b + 4)
                        turn_pv(b, 0)
                        scores(b, q, 13)
                        scores(b, q, 14)
                        weigh(b, q, 3)
                        for u in (15, 16, 17):
                            scores(b, q, u)
                            if not last:
                                for r in range(3 * (u - 15), min(3 * (u - 15) + 3, 8)):
                                    turn_qk(b + 1, 1 - q, r)
                    pairs(e, body, ahead=True, behind=True)
                    weigh(B - 1, 1, 4)
                    weigh(B - 1, 1, 5)
                    turn_pv(B - 1, 1)
                    turn_att(B - 1)
                    out_rows(B - 1)
                elif stage == "toep":
                    stage_gate(e, stage)
                    for v, m0 in enumerate((0, 4, 5)):
                        for h in range(2):
                            m = {0: (0, 1), 4: (4, 3), 5: (5, 1)}[m0][h]
                            dst = bank(v)[:, 256 * h:256 * h + 256].rearrange("p (w c) -> p w c", w=2)
                            for k in range(2):
                                ins = e.matmul(dst, dft_f[:, k, P * m:P * m + P], t_in[:, k:NT:2, :], start=(k == 0), stop=(k == 1))
                    ins.then_inc(s("kernel_bank"), 1)
                    e.wait_ge(s("kernel_ready"), 1)

                    def forward(b, q):
                        e.wait_ge(s("z_ready"), B * upd[stage] + b + 1)
                        e.wait_ge(s("toep_bank_free"), b + 1)
                        for m in range(4):
                            dst = bank(2 * q, 2)[:, 256 * m:256 * m + 256].rearrange("p (w c) -> p w c", w=2)
                            for k in range(2):
                                ins = e.matmul(dst, dft_f[:, k, P * m:P * m + P], z[q][:, k:NT:2, :], start=(k == 0), stop=(k == 1))
                        ins.then_inc(s("toep_z_used"), 1)

                    def inverse(b, q):
                        e.wait_ge(s("toep_spec"), b + 1)
                        for k in range(2):
                            dst = bank(4 + q)[:, 256 * k:256 * k + 256]
                            for m in range(4):
                                ins = e.matmul(dst, dft_i[:, m, P * k:P * k + P],
                                               yf[q][:, m // 2, m % 2, :, :].rearrange("p w c -> p (w c)"),
                                               start=(m == 0), stop=(m == 3))
                        ins.then_inc(s("toep_out"), 1)
                    forward(0, 0)

                    def body(b, q):
                        if not (isinstance(b, int) and b == B - 1):
                            forward(b + 1, 1 - q)
                        inverse(b, q)
                    pairs(e, body, ahead=True)
                elif stage in ("mix0", "mix1"):
                    mb = 0 if stage == "mix0" else B
                    stage_gate(e, stage)

                    def front(b, q):
                        turn_z(e, stage, b, q)

                    def keys(b, q):
                        e.wait_ge(s("mix_xk"), mb + b + 1)
                        e.wait_ge(s("mix_k_free"), mb + b + 1)
                        e.matmul(bank(q), w_k[:, :], xkT[q][:, :], start=True, stop=True).then_inc(s("mix_k"), 1)
                        e.wait_ge(s("mix_r_free"), mb + b + 1)
                        for i in range(NT):
                            ins = e.matmul(bank(2 + q)[:, C * i:C * i + C], xrT[q][:, P * i:P * i + P], w_r[:, :], start=True, stop=True)
                        ins.then_inc(s("mix_r"), 1)

                    def values(b, q):
                        e.wait_ge(s("mix_kact"), mb + b + 1)
                        if not (isinstance(b, int) and b < 2):
                            e.wait_ge(s("mix_gated"), mb + b - 1)
                        for i in range(NT):
                            ins = e.matmul(bank(4 + q)[:, C * i:C * i + C], kact[q][:, P * i:P * i + P], w_v[:, :], start=True, stop=True)
                        ins.then_inc(s("mix_v"), 1)
                    front(0, 0)

                    def body(b, q):
                        if not (isinstance(b, int) and b == B - 1):
                            front(b + 1, 1 - q)
                        keys(b, q)
                        values(b, q)
                    pairs(e, body, ahead=True, behind=True)
                elif stage == "scan":
                    stage_gate(e, stage)
                    e.wait_ge(s("scan_const"), 1)
                    for m in range(MI):
                        for j in range(MI):
                            e.matmul(bank(5)[:, C * m:C * m + C], w_d[:, j, P * m:P * m + P], w_out[:, j, :],
                                     start=(j == 0), stop=(j == MI - 1))
                    for j in range(MI):
                        e.matmul(bank(4)[:, 0:C], decay_row[:, j, 0:P], w_out[:, j, :], start=(j == 0), stop=False)
                    e.matmul(bank(4)[:, 0:C], decay_row[0:1, 0, P:2 * P], out_b_row[:, :], start=False, stop=True) \
                        .then_inc(s("scan_fold"), 1)
                    e.wait_ge(s("scan_ready"), 1)

                    def gates(b, q):
                        e.wait_ge(s("turn_bank_free"), B * turn[stage] + b + 3)
                        for m in range(MI):
                            if not (isinstance(b, int) and b < 1):
                                e.wait_ge(s("u_ready"), MI * (b - 1) + m + 1)
                            e.matmul(bank(2 * m), w_in[:, P * m:P * m + P], xrT[q][:, :], start=True, stop=True)
                            e.matmul(bank(2 * m + 1), w_gate[:, P * m:P * m + P], xrT[q][:, :], start=True, stop=True) \
                                .then_inc(s("ug"), 1)

                    def states(b, q):
                        e.wait_ge(s("u_ready"), MI * b + MI)
                        for m in range(MI):
                            e.wait_ge(s("b_free"), MI * b + m + 1)
                            for j in range(MI):
                                ins = e.matmul(bank(4), w_b[:, j, P * m:P * m + P], uT[q][:, j, :], start=(j == 0), stop=(j == MI - 1))
                            ins.then_inc(s("b_bank"), 1)
                            if not (isinstance(b, int) and b == 0 and m == 0):
                                e.wait_ge(s("ch_ready"), MI * b + m)
                            for j in range(MI):
                                ins = e.matmul(bank(5), w_c[:, j, P * m:P * m + P], uT[q][:, j, :], start=(j == 0), stop=(j == MI - 1))
                            ins.then_inc(s("c_bank"), 1)

                    def outs(b, q):
                        e.wait_ge(s("ch_ready"), MI * b + MI)
                        e.wait_ge(s("x_updated"), B * upd[stage] + b)
                        for i in range(NT):
                            for j in range(MI):
                                e.matmul(bank(7)[:, C * i:C * i + C], uT[q][:, j, P * i:P * i + P], w_od[:, j, :],
                                         start=(j == 0), stop=False)
                            for j in range(MI):
                                ins = e.matmul(bank(7)[:, C * i:C * i + C], chT[q][:, j, P * i:P * i + P], w_out[:, j, :],
                                               start=False, stop=(j == MI - 1))
                        ins.then_inc(s("o_bank"), 1)

                    def turn6(b, q):
                        e.wait_ge(s("z_ready"), B * upd[stage] + b + 1)
                        e.wait_ge(s("turn_bank_free"), B * turn[stage] + b + 2)
                        for i in range(NT):
                            ins = e.transpose(bank(6)[:, P * i:P * i + P], z[q][:, i, :], ident[:, :])
                        ins.then_inc(s("turned"), 1)
                    turn6(0, 0)
                    gates(0, 0)

                    def body(b, q):
                        last = isinstance(b, int) and b == B - 1
                        if not last:
                            turn6(b + 1, 1 - q)
                        states(b, q)
                        if not last:
                            gates(b + 1, 1 - q)
                        outs(b, q)
                    pairs(e, body, ahead=True, behind=True)

        @block.scalar
        def _(e):
            for name, n in (("turn_bank_free", 2), ("mix_k_free", 2), ("mix_r_free", 2), ("b_free", 1)):
                e.sem_inc(s(name), n)
            e.wait_ge(s("weights"), 16 * N_LOAD)
            if "conv" in stages:
                e.preload_act_table(ACT.Exp)
                e.wait_ge(s("conv_y"), 1)

                def front(n, q):
                    if not (isinstance(n, int) and n < 2):
                        at(e, "yT_bank", n - 1)
                    e.copy(y_cur[q][:, :], y_ext[:, own(n, REACH * C)]).then_inc(s("y_cur"), 1)
                    e.wait_ge(s("yT_bank"), n + 1)
                    if not (isinstance(n, int) and n < 2):
                        e.wait_ge(s("logits"), n - 1)
                    e.copy(yT_cur[q][:, :], bank(q)[:, 0:P]).then_inc(s("yT_cur"), 1)

                def expo_w(n, q):
                    e.wait_ge(s("conv_sub"), n + 1)
                    e.wait_ge(s("prod_free"), n + 1)
                    e.activation(e_w[q][:, :], logit[q][:, :], ACT.Exp).then_inc(s("conv_e"), 1)

                front(0, 0)
                front(1, 1)

                def body(n, q):
                    expo_w(n, q)
                    if not (isinstance(n, int) and n >= OWN - 2):
                        front(n + 2, q)
                pairs(e, body, ahead=True, count=OWN)
            for stage in ln_stages:
                if stage in ("ffn0", "ffn1"):
                    fb = 0 if stage == "ffn0" else B

                    def body(b, q):
                        at(e, "turned", B * turn[stage] + b + 1)
                        e.activation(xnT[:, tok(b)], bank(6 + q), ACT.Identity, bias=gam_beta[:, 1:2], scale=gam_beta[:, 0:1]) \
                            .then_inc(s("turn_bank_free"), 1)
                    pairs(e, body)
                elif stage == "attn":
                    e.preload_act_table(ACT.Exp)
                    stage_gate(e, stage)
                    nt = B * turn[stage]
                    e.wait_ge(s("zT_zero"), 2)

                    def copy_z(b, q):
                        e.wait_ge(s("turned"), nt + b + 1)
                        if not (isinstance(b, int) and b < 2):
                            e.wait_ge(s("v_bank"), b - 1)
                        e.copy(zT[q][:, 1:1 + T], bank(5)).then_inc(s("turn_bank_free"), 1)

                    def copy_coord(b, q, v):
                        e.wait_ge(s("coord_bank"), 2 * b + v + 1)
                        if not (isinstance(b, int) and b == 0) and v == 0:
                            e.wait_ge(s("lines"), b)
                        for side in range(2):
                            src = bank(5 + v).rearrange("p (i s f) -> p i s f", i=NT, s=2)[:, :, side, :]
                            dst = coord[:, v, side * NT * HEADS:(side + 1) * NT * HEADS, 0:4].rearrange("p (i h) c -> p i h c", i=NT)
                            ins = e.copy(dst, src.rearrange("p i (h c) -> p i h c", c=4))
                        ins.then_inc(s("coord_copied"), 1)

                    def copy_v(b, q):
                        e.wait_ge(s("v_bank"), b + 1)
                        if not (isinstance(b, int) and b < 2):
                            e.wait_ge(s("weighed"), CHUNKS * (b - 1))
                        for half in range(2):
                            e.copy(v_pair[q][KB * half:KB * half + KB, :, :, 16 * half:16 * half + D_HEAD],
                                   bank(5)[KB * half:KB * half + KB, :].rearrange("p (j a d) -> p j a d", j=NJ, d=D_HEAD)) \
                                .then_inc(s("v_copied"), 1)

                    def expo_u(b, q, u):
                        g, c, i0 = u // 9, min(u % 9 // 4, 2), u % 9 % 4
                        k = 3 * g + c
                        if i0 == 0 and not (isinstance(b, int) and b == 0 and k < 3):
                            e.wait_ge(s("weighed"), CHUNKS * b + k - 2)
                        e.wait_ge(s("scored"), UNITS * b + u + 1)
                        dst = probs_c2[:, :, :].rearrange("p a b -> p (a b)") if c == 2 else probs[c][:, i0, :]
                        e.activation(dst, bank(2 * (u % 2), 2), ACT.Exp, scale=SCALE).then_inc(s("p_ready"), 1)

                    def copy_att(b):
                        e.wait_ge(s("att_turned"), b + 1)
                        if not (isinstance(b, int) and b == 0):
                            e.wait_ge(s("att_out"), b)
                        e.copy(attT[:, :], bank(5)).then_inc(s("aT_copied"), 1)

                    copy_z(0, 0)
                    copy_coord(0, 0, 0)
                    copy_coord(0, 0, 1)
                    e.wait_ge(s("attn_init"), 1)
                    copy_v(0, 0)

                    def body(b, q):
                        first, last = (isinstance(b, int) and b == x for x in (0, B - 1))
                        for u in range(UNITS):
                            expo_u(b, q, u)
                            if u == 4 and not first:
                                copy_att(b - 1)
                            if not last:
                                if u == 6:
                                    copy_z(b + 1, 1 - q)
                                if u in (7, 8):
                                    copy_coord(b + 1, 1 - q, u - 7)
                                if u == 10:
                                    copy_v(b + 1, 1 - q)
                    pairs(e, body, ahead=True, behind=True)
                    copy_att(B - 1)
                elif stage == "toep":
                    pass
                elif stage in ("mix0", "mix1"):
                    mb = 0 if stage == "mix0" else B
                    e.preload_act_table(ACT.Sigmoid)
                    stage_gate(e, stage)
                    e.wait_ge(s("zT_zero"), 2)

                    def front(b, q):
                        e.wait_ge(s("turned"), B * turn[stage] + b + 1)
                        if not (isinstance(b, int) and b < 2):
                            e.wait_ge(s("mix_xk"), mb + b - 1)
                        e.copy(zT[q][:, 1:1 + T], bank(6 + q)).then_inc(s("turn_bank_free"), 1)

                    def rest(b, q):
                        e.wait_ge(s("mix_k"), mb + b + 1)
                        if not (isinstance(b, int) and b < 2):
                            e.wait_ge(s("mix_v"), mb + b - 1)
                        e.activation(kact[q][:, :], bank(q), ACT.Relu).then_inc(s("mix_k_free"), 1)
                        e.drain()
                        e.square(kact[q][:, :], kact[q][:, :]).then_inc(s("mix_kact"), 1)
                        e.wait_ge(s("mix_r"), mb + b + 1)
                        if not (isinstance(b, int) and b < 2):
                            e.wait_ge(s("mix_gated"), mb + b - 1)
                        e.activation(rsig[q][:, :], bank(2 + q), ACT.Sigmoid).then_inc(s("mix_r_free"), 1)
                    front(0, 0)

                    def body(b, q):
                        if not (isinstance(b, int) and b == B - 1):
                            front(b + 1, 1 - q)
                        rest(b, q)
                    pairs(e, body, ahead=True, behind=True)
                elif stage == "scan":
                    stage_gate(e, stage)
                    e.activation(decay[:, :], vecs[:, 5, :], ACT.Sigmoid, scale=-1.0).then_inc(s("scan_decay"), 1)

                    def front(b, q):
                        e.wait_ge(s("turned"), B * turn[stage] + b + 1)
                        if not (isinstance(b, int) and b < 2):
                            e.wait_ge(s("ug"), MI * (b - 1))
                        e.activation(xrT[q][:, :], bank(6), ACT.Copy, scale=norm_w[:, 0:1]).then_inc(s("turn_bank_free"), 1)

                    def gate_sig(b, q):
                        for m in range(MI):
                            e.wait_ge(s("ug"), MI * b + m + 1)
                            if not (isinstance(b, int) and b < 1):
                                e.wait_ge(s("u_ready"), MI * (b - 1) + m + 1)
                            e.activation(gate[m][:, :], bank(2 * m + 1), ACT.Sigmoid, bias=vecs[:, 1, m:m + 1]).then_inc(s("gate"), 1)

                    def b_copy(b, q):
                        for m in range(MI):
                            e.wait_ge(s("b_bank"), MI * b + m + 1)
                            if not (isinstance(b, int) and b < 1):
                                e.wait_ge(s("h_ready"), MI * (b - 1) + m + 1)
                            e.activation(bT[m][:, :], bank(4), ACT.Identity, bias=vecs[:, 2, m:m + 1]).then_inc(s("b_free"), 1)
                    front(0, 0)
                    gate_sig(0, 0)

                    def body(b, q):
                        last = isinstance(b, int) and b == B - 1
                        if not last:
                            front(b + 1, 1 - q)
                        b_copy(b, q)
                        if not last:
                            gate_sig(b + 1, 1 - q)
                    pairs(e, body, ahead=True, behind=True)

        @block.vector
        def _(e):
            e.wait_ge(s("weights"), 16 * N_LOAD)
            e.sem_inc(s("toep_bank_free"), 2)
            if "conv" in stages:
                for half, name in enumerate(("x_blk_lo", "x_blk_hi")):
                    e.wait_ge(s(name), 16)
                    for t in range(half * OWN // 2, (half + 1) * OWN // 2):
                        e.bn_stats(st_c[:, t, :], x_blk[:, t * C:t * C + C])
                e.drain()
                for t in range(OWN):
                    e.bn_aggr(mv_c[:, t, :], st_c[:, t, :])
                e.drain()
                e.tensor_scalar(arg_c[:, :], mv_c[:, :, 1], LN_EPS, None, ALU.add).then_inc(s("conv_var"), 1)
                e.wait_ge(s("conv_rstd"), 1)
                for t in range(OWN):
                    ins = e.tensor_scalar(y_ext[:, (REACH + t) * C:(REACH + t + 1) * C], x_blk[:, t * C:t * C + C],
                                          mv_c[:, t, 0:1], rstd_c[:, t:t + 1], ALU.subtract, ALU.mult)
                ins.then_inc(s("conv_y"), 1)

                def hk(ap):
                    return ap.rearrange("p (k h) -> p h k", h=HEADS)

                def front(n, q):
                    at(e, "logits", n + 1)
                    e.tensor_reduce(mx[q][:, :], hk(bank(2 + q)[:, 0:TAPS * HEADS]), AX.X, ALU.max)
                    e.drain()
                    e.tensor_tensor(hk(logit[q][:, :]), hk(bank(2 + q)[:, 0:TAPS * HEADS]),
                                    mx[q][:, :].unsqueeze(2).to_broadcast([P, HEADS, TAPS]), ALU.subtract).then_inc(s("conv_sub"), 1)

                def products(n, q):
                    e.wait_ge(s("conv_e"), n + 1)
                    e.tensor_reduce(esum[q][:, :], hk(e_w[q][:, :]), AX.X, ALU.add)
                    at(e, "prod_free", n + 1)
                    k1 = TAPS - POOL_TAPS
                    e.tensor_tensor(prod[q][:, 0:k1 * C].rearrange("p (k h r) -> p k h r", h=HEADS, r=R),
                                    y_ext[:, window(n, 0, k1)].rearrange("p (k h r) -> p k h r", h=HEADS, r=R),
                                    e_w[q][:, 0:k1 * HEADS].rearrange("p (k h) -> p k h", h=HEADS).unsqueeze(3)
                                    .to_broadcast([P, k1, HEADS, R]), ALU.mult).then_inc(s("prod_vec"), 1)
                    e.drain()
                    e.reciprocal(erec[q][:, :], esum[q][:, :])

                def average(n, q):
                    at(e, "prod_free", n + 3)
                    if not (isinstance(n, int) and n < 2):
                        at(e, "conv_x", n - 1)
                    e.tensor_tensor(avg[q][:, :].rearrange("p (h r) -> p h r", r=R),
                                    bank(4 + q)[:, 0:C].rearrange("p (h r) -> p h r", r=R),
                                    erec[q][:, :].unsqueeze(2).to_broadcast([P, HEADS, R]), ALU.mult).then_inc(s("conv_avg"), 1)

                e.wait_ge(s("halo"), 16 * B)
                e.sem_inc(s("prod_free"), 2)
                front(0, 0)
                front(1, 1)
                products(0, 0)
                products(1, 1)
                average(0, 0)
                front(2, 0)
                with e.Fori(2, OWN - 3, 2) as n:
                    front(n + 1, 1)
                    products(n, 0)
                    average(n - 1, 1)
                    front(n + 2, 0)
                    products(n + 1, 1)
                    average(n, 0)
                front(OWN - 1, 1)
                products(OWN - 2, 0)
                average(OWN - 3, 1)
                products(OWN - 1, 1)
                e.drain()
                average(OWN - 2, 0)
                average(OWN - 1, 1)

            if "ffn0" in stages:
                e.tensor_reduce(w_beta[:, 0:1], w_raw[:, :], AX.X, ALU.add, apply_absolute_value=True).then_inc(s("w_abs"), 1)
                e.wait_ge(s("w_mean"), 1)
                e.tensor_copy(w_beta[:, 1:2], bank(5)[:, 0:1])
                e.drain()
                e.tensor_scalar(w_beta[:, 2:3], w_beta[:, 1:2], LN_EPS, None, ALU.add)
                e.drain()
                e.tensor_scalar(w_beta[:, 2:3], w_beta[:, 2:3], 0.5, None, ALU.mult)
                e.drain()
                e.tensor_scalar(w_beta[:, 3:4], w_beta[:, 2:3], -1.0, None, ALU.mult)
                e.tensor_scalar(w_q[:, :], w_raw[:, :], w_beta[:, 2:3], None, ALU.is_gt)
                e.drain()
                e.tensor_scalar(w_scr[:, :], w_raw[:, :], w_beta[:, 3:4], None, ALU.is_lt)
                e.drain()
                e.tensor_tensor(w_q[:, :], w_q[:, :], w_scr[:, :], ALU.subtract)
                e.drain()

            for stage in ln_stages:
                fac, add = LN_CONST[kind[stage]]
                if stage in ("ffn0", "ffn1"):
                    fb = 0 if stage == "ffn0" else B
                    ln_stats(e, stage, 0, 0, fac, add)
                    ln_norm(e, stage, 0, 0)

                    def body(b, q):
                        last = isinstance(b, int) and b == B - 1
                        if not last:
                            ln_stats(e, stage, b + 1, 1 - q, fac, add)
                        at(e, "turn_bank_free", B * turn[stage] + b + 3)
                        dst = amax[:, b:b + 1] if isinstance(b, int) else amax[:, bass.ds(b, 1)]
                        e.tensor_reduce(dst, xnT[:, tok(b)], AX.X, ALU.max, apply_absolute_value=True)
                        if not last:
                            ln_norm(e, stage, b + 1, 1 - q)
                    pairs(e, body, ahead=True)
                    e.drain()
                    e.tensor_reduce(amax1[:, :], amax[:, :], AX.X, ALU.max).then_inc(s("amax"), 1)
                    e.wait_ge(s("gmax"), 1 if stage == "ffn0" else 2)
                    e.tensor_scalar(bound[:, 0:1], gmax[:, :], CLIP, None, ALU.mult)
                    e.tensor_scalar(bound[:, 1:2], gmax[:, :], -CLIP, None, ALU.mult)
                    e.drain()

                    def clip(b, q):
                        if not (isinstance(b, int) and b < 2):
                            at(e, "ffn_y", fb + b - 1)
                        e.tensor_scalar(clipped[q][:, :], xnT[:, tok(b)], bound[:, 0:1], bound[:, 1:2], ALU.min, ALU.max) \
                            .then_inc(s("clipped"), 1)

                    def add_y(b, q):
                        at(e, "ffn_y", fb + b + 1)
                        e.scalar_tensor_tensor(x_tile[:, tok(b)], bank(q), w_beta[:, 1:2], x_tile[:, tok(b)], ALU.mult, ALU.add) \
                            .then_inc(s("x_updated"), 1)
                    clip(0, 0)
                    clip(1, 1)

                    def body(b, q):
                        add_y(b, q)
                        if not (isinstance(b, int) and b >= B - 2):
                            clip(b + 2, q)
                    pairs(e, body, ahead=True)
                elif stage == "attn":
                    stage_gate(e, stage)
                    e.tensor_copy(b_v_wide[:, :], b_v[:, 0:1].to_broadcast([P, P]))
                    e.tensor_copy(ident_b[:, :], ident[:, :])
                    e.drain().then_inc(s("b_v_wide"), 1)
                    ln_stats(e, stage, 0, 0, fac, add)
                    e.wait_ge(s("bias_bank"), 1)
                    e.tensor_copy(att_bias[:, :], bank(4)[:, 0:C]).then_inc(s("att_bias"), 1)
                    ln_norm(e, stage, 0, 0)
                    ln_stats(e, stage, 1, 1, fac, add)

                    def lines(b, q):
                        e.wait_ge(s("coord_copied"), 2 * b + 2)
                        e.tensor_copy(coord[:, :, :, 4:6].rearrange("p v g c -> p (v g) c"), coord[:, :, :, 1:3].rearrange("p v g c -> p (v g) c"))
                        pa, pb = (coord[:, v, :, :].rearrange("p (s g) c -> p s g c", s=2) for v in range(2))
                        shape = [P, 2, NT * HEADS, 3]

                        def star(m):
                            return triple(m, 0, 3)

                        def tri(m):
                            return triple(m, 3, -3)

                        def triple(m, start, shift):
                            v = m[:, :, :, start:start + 3]
                            (ps_, pn), (ss, sn), (gs, gn), (cs, cn) = v.ap
                            return bass.AP(v.tensor, v.offset, [[ps_, pn], [ss + shift, sn], [gs, gn], [cs, cn]])
                        e.tensor_tensor(star(m_a), pa[:, :, :, 0:1].to_broadcast(shape), pb[:, :, :, 1:4], ALU.mult)
                        e.tensor_tensor(star(m_b), pb[:, :, :, 0:1].to_broadcast(shape), pa[:, :, :, 1:4], ALU.mult)
                        e.drain()
                        e.tensor_tensor(tri(m_a), pa[:, :, :, 2:5], pb[:, :, :, 3:6], ALU.mult)
                        e.tensor_tensor(tri(m_b), pb[:, :, :, 2:5], pa[:, :, :, 3:6], ALU.mult)
                        e.drain().then_inc(s("lines"), 1)
                        e.tensor_tensor(line[:, :, :, :], m_a[:, :, :, :], m_b[:, :, :, :], ALU.subtract)
                        e.drain()
                        e.tensor_tensor(m_a[:, :, :, :], line[:, :, :, :], line[:, :, :, :], ALU.mult)
                        e.drain()
                        e.tensor_reduce(len2[:, :], m_a[:, :, :, :].rearrange("p s g c -> p (s g) c"), AX.X, ALU.add)
                        e.drain()
                        e.tensor_scalar(len2[:, :], len2[:, :], 1e-24, None, ALU.max).then_inc(s("len2"), 1)

                    def split(b, q):
                        e.wait_ge(s("inv_len"), b + 1)
                        lv = line[:, :, :, :].rearrange("p s g c -> p (s g) c")
                        e.tensor_tensor(lv, lv, inv_len[:, :].unsqueeze(2).to_broadcast([P, 2 * NT * HEADS, COMPS]), ALU.mult)
                        e.drain()
                        if not (isinstance(b, int) and b == 0):
                            e.wait_ge(s("qk_turned"), 8 * b)
                        sides = ((split_q, slice(0, 3), slice(3, 5), 5), (split_k, slice(1, 6, 2), slice(2, 5, 2), 0))
                        sv = [sp[:, :, 0:SLOTS * COMPS].rearrange("p g (t c) -> p g t c", c=COMPS) for sp, *_ in sides]
                        for n, (sp, hs, ms, ls) in enumerate(sides):
                            e.tensor_copy(sv[n][:, :, hs, :], line[:, n, :, :].unsqueeze(2).to_broadcast([P, NT * HEADS, 3, COMPS]))
                        e.drain()
                        for n, (sp, hs, ms, ls) in enumerate(sides):
                            e.tensor_tensor(rest[:, n, :, :], line[:, n, :, :], sv[n][:, :, 1, :], ALU.subtract)
                        e.drain()
                        for n, (sp, hs, ms, ls) in enumerate(sides):
                            e.tensor_copy(sv[n][:, :, ms, :], rest[:, n, :, :].unsqueeze(2).to_broadcast([P, NT * HEADS, 2, COMPS]))
                        e.drain()
                        for n, (sp, hs, ms, ls) in enumerate(sides):
                            e.tensor_tensor(sv[n][:, :, ls, :], rest[:, n, :, :], sv[n][:, :, 4, :], ALU.subtract).then_inc(s("split"), 1)

                    def copy_qk(b, q, r):
                        e.wait_ge(s("qk_turned"), 8 * b + r + 1)
                        p0 = 2 * (r // 2)
                        src = bank(7).bitcast(BF16)
                        if r % 2 == 0:
                            e.tensor_copy(qT[q][0:QK_ROWS, p0:p0 + 2, :].rearrange("p a t -> p (a t)"), src[0:QK_ROWS, 0:2 * T]) \
                                .then_inc(s("qk_copied"), 1)
                        else:
                            for half in range(2):
                                rows = slice(ROWS_B * half, ROWS_B * half + SLOTS * COMPS)
                                ins = e.tensor_copy(kT[q][rows, p0:p0 + 2, :, KB * half:KB * half + KB].rearrange("p a j t -> p (a j) t"),
                                                    src[rows, 0:2 * T].rearrange("p (a t) -> p a t", t=KB))
                            ins.then_inc(s("qk_copied"), 1)

                    def copy_pv(b, g):
                        e.wait_ge(s("weighed"), CHUNKS * b + 3 * g + 3)
                        if not (isinstance(b, int) and b == 0 and g == 0):
                            e.wait_ge(s("pv_turned"), 2 * b + g)
                        e.tensor_copy(pv_sb[:, :], bank(4)).then_inc(s("pv_copied"), 1)

                    def norm_att(b, g):
                        e.drain()
                        e.wait_ge(s("pv_turned"), 2 * b + g + 1)
                        pv = bank(6).rearrange("p (i h v) -> p i h v", i=NT, v=16)
                        e.reciprocal(inv_den[:, :, :], pv[:, :, :, D_HEAD])
                        e.drain()
                        if g == 0 and not (isinstance(b, int) and b == 0):
                            e.wait_ge(s("att_turned"), b)
                        for i in range(NT):
                            ins = e.tensor_tensor(att[:, i, 64 * g:64 * g + 64].rearrange("p (h v) -> p h v", v=D_HEAD), pv[:, i, :, 0:D_HEAD],
                                                  inv_den[:, i, :].unsqueeze(2).to_broadcast([P, 8, D_HEAD]), ALU.mult)
                        ins.then_inc(s("att_ready"), 1)

                    def add_att(b):
                        e.wait_ge(s("x_biased"), b + 1)
                        at(e, "att_out", b + 1)
                        e.tensor_tensor(x_tile[:, tok(b)], bank(6), x_tile[:, tok(b)], ALU.add).then_inc(s("x_updated"), 1)

                    lines(0, 0)
                    ln_norm(e, stage, 1, 1)
                    e.wait_ge(s("attn_init"), 1)
                    split(0, 0)
                    for r in range(8):
                        copy_qk(0, 0, r)

                    def body(b, q):
                        first, last = (isinstance(b, int) and b == x for x in (0, B - 1))
                        if not first:
                            copy_pv(b - 1, 1)
                            norm_att(b - 1, 1)
                            add_att(b - 1)
                        if not (isinstance(b, int) and b >= B - 2):
                            ln_stats(e, stage, b + 2, q, fac, add)
                        if not last:
                            lines(b + 1, 1 - q)
                        copy_pv(b, 0)
                        if not last:
                            split(b + 1, 1 - q)
                        norm_att(b, 0)
                        if not (isinstance(b, int) and b >= B - 2):
                            ln_norm(e, stage, b + 2, q)
                        if not last:
                            for r in range(8):
                                copy_qk(b + 1, 1 - q, r)
                    pairs(e, body, ahead=True, behind=True)
                    copy_pv(B - 1, 1)
                    norm_att(B - 1, 1)
                    add_att(B - 1)
                elif stage == "toep":
                    stage_gate(e, stage)
                    e.wait_ge(s("kernel_bank"), 1)
                    for v in range(3):
                        src = bank(v).rearrange("p (h w c) -> p h w c", h=2, w=2)
                        e.tensor_copy(kf[0][:, v, :, :], src[:, :, 0, :])
                        e.drain()
                        ins = e.scalar_tensor_tensor(kf[1][:, v, :, :], kf[0][:, v, :, :], sgn[:, 0:1], src[:, :, 1, :], ALU.mult, ALU.add)
                    ins.then_inc(s("kernel_ready"), 1)
                    e.drain()
                    ln_stats(e, stage, 0, 0, fac, add)
                    ln_norm(e, stage, 0, 0)

                    def body(b, q):
                        last = isinstance(b, int) and b == B - 1
                        if not last:
                            ln_stats(e, stage, b + 1, 1 - q, fac, add)
                        e.drain()
                        e.wait_ge(s("toep_z_used"), b + 1)
                        re, im = (bank(2 * q + v).rearrange("p (h w c) -> p h w c", h=2, w=2) for v in range(2))

                        def k0(v):
                            return kf[0][:, v, :, :].unsqueeze(2).to_broadcast([P, 2, 2, C])
                        for n, (src, v) in enumerate(((re, 0), (im, 1), (re, 1), (im, 2))):
                            ins = e.tensor_tensor(pu[n][:, :, :], src[:, :, 0, :], kf[1][:, v, :, :], ALU.mult)
                        ins.then_inc(s("toep_pu"), 1)
                        for n, (src, v) in enumerate(((re, 0), (im, 1), (re, 1), (im, 2))):
                            ins = e.tensor_tensor(pr[n][:, :, :, :], src, k0(v), ALU.mult)
                        ins.then_inc(s("toep_bank_free"), 1)
                        if not last:
                            ln_norm(e, stage, b + 1, 1 - q)
                        e.drain()
                        if not (isinstance(b, int) and b < 2):
                            e.wait_ge(s("toep_out"), b - 1)
                        e.tensor_tensor(yf[q][:, 0, :, :, :], pr[0][:, :, :, :], pr[1][:, :, :, :], ALU.subtract)
                        e.tensor_tensor(yf[q][:, 1, :, :, :], pr[2][:, :, :, :], pr[3][:, :, :, :], ALU.add)
                        e.drain()
                        e.wait_ge(s("toep_cross"), b + 1)
                        e.tensor_tensor(yf[q][:, 0, :, 1, :], yf[q][:, 0, :, 1, :], pu[0][:, :, :], ALU.add)
                        e.tensor_tensor(yf[q][:, 1, :, 1, :], yf[q][:, 1, :, 1, :], pu[2][:, :, :], ALU.add).then_inc(s("toep_spec"), 1)
                        if not (isinstance(b, int) and b == 0):
                            res(b - 1, 1 - q)

                    def res(b, q):
                        at(e, "toep_out", b + 1)
                        xv = x_tile[:, tok(b)].rearrange("p (w k c) -> p k w c", w=2, k=2)
                        e.tensor_tensor(xv, bank(4 + q).rearrange("p (k w c) -> p k w c", w=2, k=2), xv, ALU.add) \
                            .then_inc(s("x_updated"), 1)
                    pairs(e, body, ahead=True, behind=True)
                    res(B - 1, 1)
                elif stage in ("mix0", "mix1"):
                    mb = 0 if stage == "mix0" else B
                    ln_stats(e, stage, 0, 0, fac, add)
                    ln_norm(e, stage, 0, 0)
                    ln_stats(e, stage, 1, 1, fac, add)

                    def mix(b, q):
                        e.wait_ge(s("turn_bank_free"), B * turn[stage] + b + 3)
                        e.tensor_tensor(dif[q][:, :], zT[q][:, 1:1 + T], zT[q][:, 0:T], ALU.subtract)
                        e.drain()
                        if not (isinstance(b, int) and b < 2):
                            e.wait_ge(s("mix_r"), mb + b - 1)
                        e.scalar_tensor_tensor(xrT[q][:, :], dif[q][:, :], mus[:, 0:1], zT[q][:, 0:T], ALU.mult, ALU.add)
                        e.scalar_tensor_tensor(xkT[q][:, :], dif[q][:, :], mus[:, 1:2], zT[q][:, 0:T], ALU.mult, ALU.add) \
                            .then_inc(s("mix_xk"), 1)

                    def gated_v(b, q):
                        e.wait_ge(s("mix_v"), mb + b + 1)
                        e.wait_ge(s("mix_r_free"), mb + b + 3)
                        if not (isinstance(b, int) and b < 2):
                            e.wait_ge(s("x_updated"), B * upd[stage] + b - 1)
                        e.tensor_tensor(gated[q][:, :], bank(4 + q), rsig[q][:, :], ALU.mult).then_inc(s("mix_gated"), 1)

                    mix(0, 0)

                    def body(b, q):
                        if not (isinstance(b, int) and b == B - 1):
                            ln_norm(e, stage, b + 1, 1 - q)
                            if not (isinstance(b, int) and b == B - 2):
                                ln_stats(e, stage, b + 2, q, fac, add)
                            mix(b + 1, 1 - q)
                        gated_v(b, q)
                    pairs(e, body, ahead=True, behind=True)
                elif stage == "scan":
                    stage_gate(e, stage)
                    ln_stats(e, stage, 0, 0, fac, add, extra=True)
                    ln_norm(e, stage, 0, 0)
                    for j in range(MI):
                        e.memset(decay_row[:, j, 0:2 * P], 1.0)
                    e.drain()
                    for j in range(MI):
                        ins = e.tensor_scalar(decay_row[:, j, 0:P], decay_row[:, j, 0:P], vecs[:, 4, j:j + 1], None, ALU.mult)
                    ins.then_inc(s("scan_const"), 1)
                    e.wait_ge(s("scan_fold"), 1)
                    e.tensor_copy(w_od[:, :, :].rearrange("p m c -> p (m c)"), bank(5)[:, 0:MI * C])
                    e.tensor_copy(bias_row[:, :], bank(4)[:, 0:C])
                    for j in range(MI):
                        e.memset(decay_row[:, j, :], 1.0)
                    e.drain()
                    e.wait_ge(s("scan_decay"), 1)
                    for j in range(MI):
                        ins = e.tensor_scalar(decay_row[:, j, :], decay_row[:, j, :], decay[:, j:j + 1], None, ALU.mult)
                    ins.then_inc(s("scan_ready"), 1)
                    e.drain()

                    def u_mul(b, q):
                        for m in range(MI):
                            e.wait_ge(s("gate"), MI * b + m + 1)
                            if not (isinstance(b, int) and b < 2):
                                e.wait_ge(s("o_bank"), b - 1)
                            e.scalar_tensor_tensor(uT[q][:, m, :], bank(2 * m), vecs[:, 0, m:m + 1], gate[m][:, :], ALU.add, ALU.mult) \
                                .then_inc(s("u_ready"), 1)

                    def first(b, q):
                        e.wait_ge(s("ratio"), b + 1)
                        e.wait_ge(s("z_ready"), B * upd[stage] + b + 1)
                        for i in range(NT):
                            e.scalar_tensor_tensor(x_plus[q][:, i * C:i * C + C], z[q][:, i, :], rstd[q][:, 1, i:i + 1],
                                                   bias_row[:, :], ALU.mult, ALU.add)

                    def h_scan(b, q):
                        for m in range(MI):
                            e.wait_ge(s("b_free"), MI * b + m + 1 + 1)
                            e.tensor_tensor_scan(hT[m][:, :], decay_row[:, m, :], bT[m][:, :], 0.0, ALU.mult, ALU.add) \
                                .then_inc(s("h_ready"), 1)
                            e.drain()
                            e.wait_ge(s("c_bank"), MI * b + m + 1)
                            if not (isinstance(b, int) and b < 2):
                                e.wait_ge(s("o_bank"), b - 1)
                            e.scalar_tensor_tensor(chT[q][:, m, :], bank(5), vecs[:, 3, m:m + 1], hT[m][:, :], ALU.add, ALU.mult) \
                                .then_inc(s("ch_ready"), 1)

                    def res(b, q):
                        e.tensor_tensor(x_plus[q][:, :], x_plus[q][:, :], x_tile[:, tok(b)], ALU.add)
                        e.drain()
                        at(e, "o_bank", b + 1)
                        e.tensor_tensor(x_tile[:, tok(b)], bank(7), x_plus[q][:, :], ALU.add).then_inc(s("x_updated"), 1)

                    u_mul(0, 0)
                    first(0, 0)

                    def body(b, q):
                        last = isinstance(b, int) and b == B - 1
                        if not last:
                            ln_stats(e, stage, b + 1, 1 - q, fac, add, extra=True)
                            ln_norm(e, stage, b + 1, 1 - q)
                            first(b + 1, 1 - q)
                        h_scan(b, q)
                        if not last:
                            u_mul(b + 1, 1 - q)
                        res(b, q)
                    pairs(e, body, ahead=True, behind=True)


def dft_tables():
    n = 2 * WIN
    t = np.arange(WIN)[:, None]
    f = np.arange(WIN)[None, :]
    ang = 2 * np.pi * ((t * f) % n) / n
    cos, sin = np.cos(ang), np.sin(ang)
    nyq = np.cos(np.pi * t)
    sin_n, cos_n = sin.copy(), cos.copy()
    sin_n[:, 0:1] = nyq
    cos_n[:, 0:1] = nyq
    fwd = np.concatenate([cos, sin_n, sin[:, :P], cos_n[:, :P]], axis=1)
    fwd = fwd.reshape(2, P, 6 * P).transpose(1, 0, 2)
    wgt = np.full((WIN, 1), 2.0 / n)
    wgt[0] = 1.0 / n
    inv = np.concatenate([cos.T * wgt, sin_n.T * wgt], axis=0)
    inv = inv.reshape(4, P, WIN).transpose(1, 0, 2)
    return np.ascontiguousarray(fwd, np.float32), np.ascontiguousarray(inv, np.float32)


def build(nc, arrays, stages=STAGES):
    d = {}
    for name, a in arrays.items():
        d[name] = nc.dram_tensor(f"in_{name}", a.shape, mybir.dt.from_np(a.dtype), kind="ExternalInput").ap()
    out = nc.dram_tensor("out_x", (B * T, C), F32, kind="ExternalOutput").ap()
    program(nc, d, out, stages)


def lay_out(i):
    g = {k: np.asarray(v) for k, v in i.items()}
    c = np.ascontiguousarray

    def by_tile(v):
        return v.reshape(MI, P).T
    fwd, inv = dft_tables()
    expo = np.empty((P, 3, NT), np.float32)
    expo[:, 0], expo[:, 1], expo[:, 2] = -0.5, 0.5, -0.5
    return {
        "x": g["L0_attn_a_x"].reshape(P, OWN * C),
        "ident": np.eye(P, dtype=np.float32),
        "w_lin": c(g["L0_attn_a_w_lin"].reshape(HEADS, TAPS, C).transpose(2, 1, 0).reshape(C, TAPS * HEADS)),
        "gam_beta": c(np.stack([g["L0_ffn_ln_gamma"], g["L0_ffn_ln_beta"]], 1)),
        "weight": g["L0_ffn_weight"],
        "dft_f": fwd, "dft_i": inv,
        "sgn": np.where(np.arange(P) % 2 == 0, 1.0, -1.0).astype(np.float32)[:, None],
        "t": c(g["L1_attn_a_t"].reshape(NT, P, C).transpose(1, 0, 2)),
        "W_r": c(g["L1_ffn_W_r"].T), "W_k": c(g["L1_ffn_W_k"].T), "W_v": c(g["L1_ffn_W_v"].T),
        "mus": c(np.stack([g["L1_ffn_mu_r"], g["L1_ffn_mu_k"]], 1)),
        "in_w": c(g["L1_attn_b_in_w"].T), "gate_w": c(g["L1_attn_b_gate_w"].T),
        "b_w": c(g["L1_attn_b_b_w"].T.reshape(MI, P, INNER).transpose(1, 0, 2)),
        "c_w": c(g["L1_attn_b_c_w"].T.reshape(MI, P, INNER).transpose(1, 0, 2)),
        "d_w": c(g["L1_attn_b_d_w"].reshape(MI, P, INNER).transpose(1, 0, 2)),
        "out_w": c(g["L1_attn_b_out_w"].T.reshape(MI, P, C).transpose(1, 0, 2)),
        "vecs": c(np.stack([by_tile(g["L1_attn_b_" + n]) for n in ("in_b", "gate_b", "b_b", "c_b", "d_b", "a_log")], 1)),
        "norm_w": c(g["L1_attn_b_norm_w"][:, None]),
        "out_b": c(g["L1_attn_b_out_b"][None, :]),
        "expo": expo,
        "w_qk": c(np.stack([np.concatenate([g["L0_attn_b_W1_q"][:C], g["L0_attn_b_W1_k"]], 1),
                            np.concatenate([g["L0_attn_b_W2_q"][:C], g["L0_attn_b_W2_k"]], 1)], 1)),
        "w_qp": c(np.stack([g["L0_attn_b_W1_q"][C:], g["L0_attn_b_W2_q"][C:]], 1)),
        "w_val": c(g["L0_attn_b_W_v"].reshape(C, PAIRS, 2, D_HEAD).transpose(0, 2, 1, 3).reshape(C, C)),
        "W_o": g["L0_attn_b_W_o"], "b_v": c(g["L0_attn_b_b_v"][:, None]), "b_o": c(g["L0_attn_b_b_o"][None, :]),
        "mask": (np.arange(KB)[None, :] >= (np.arange(P) % KB)[:, None]).astype(np.float32),
        "minus_half": np.full((P, OWN), -0.5, np.float32),
    }


def kernel(**inputs):
    import concourse.bacc as _bacc
    from concourse.bass_utils import run_bass_kernel_spmd as _run

    arrays = lay_out(inputs)
    nc = _bacc.Bacc("TRN2", target_bir_lowering=False, num_devices=1)
    build(nc, arrays)
    r = _run(nc, [{f"in_{k}": v for k, v in arrays.items()}], core_ids=[0])
    return r.results[0]["out_x"].reshape(B, T, C)
```

```python
from contextlib import ExitStack

import numpy as np
import concourse.bass as bass
from concourse import mybir

ALU = mybir.AluOpType
ACT = mybir.ActivationFunctionType
AX = mybir.AxisListType
F32 = mybir.dt.float32
BF16 = mybir.dt.bfloat16

P = 128
B, T, C = 8, 512, 128
NT = T // P
HEADS, TAPS = 16, 31
REACH = TAPS - 1
R = C // HEADS
OWN = B * T // P
PER_SEQ = T // OWN
DVE_TAPS = 13
ACT_NORM = 19
PRE_ADDED = 13
PAIRS6 = [(0, 1), (0, 2), (0, 3), (1, 2), (1, 3), (2, 3)]
D_HEAD = C // HEADS
PAIRS = HEADS // 2
KB = 64
NJ = T // KB
COMPS = 6
SLOTS = 6
ROWS_B = 64
QK_ROWS = ROWS_B + SLOTS * COMPS
SCALE = float(COMPS) ** -0.5
ROOT_SHIFT = 8
UNITS = 18
CHUNKS = 6
CHUNK_BLOCKS = ([(0, 0), (1, 512), (7, 960)], [(2, 0), (6, 384), (3, 512), (5, 832)], [(4, 0)])
D_FFN_EPS = 1e-3
LN_EPS = 1e-5
NORM_EPS = 1e-6
QUANT = 128.0
CLIP = float(np.float32(QUANT - 1e-5)) / QUANT
WIN = 256
INNER = 256
SHARED = 36600
MI = INNER // P
STAGES = ("conv", "ffn0", "attn", "ffn1", "toep", "mix0", "scan", "mix1")


def program(nc, d, out, stages=STAGES):
    ctx = ExitStack()
    with ctx:
        def sb(name, shape, dt=F32):
            return ctx.enter_context(nc.sbuf_tensor(name, shape, dt))

        def sem(name):
            return ctx.enter_context(nc.semaphore(name))

        ps = ctx.enter_context(nc.psum_tensor("ps", [P, 8 * 512], F32))

        def bank(i, n=1):
            return ps[:, 512 * i:512 * (i + n)]

        shared = sb("shared", [P, SHARED])
        cursor = [0]

        def part(shape, dt=F32):
            size = int(np.prod(shape)) * (4 if dt == F32 else 2) // 4
            a = cursor[0]
            cursor[0] += size
            assert cursor[0] <= SHARED
            v = shared[:, a:a + size]
            if dt != F32:
                v = v.bitcast(dt)
            names = "abcd"[:len(shape)]
            if len(shape) > 1:
                v = v.rearrange(f"p ({' '.join(names)}) -> p {' '.join(names)}", **dict(zip(names, shape)))
            return v

        x_tile = sb("x_tile", [P, B * NT * C])
        x_blk = part([OWN * C])
        y_ext = part([(REACH + OWN) * C])
        prod = [part([TAPS * C]) for q in range(2)]
        ident = sb("ident", [P, P])
        ident_b = sb("ident_b", [P, P], BF16)
        minus_half = sb("minus_half", [P, OWN])
        w_conv = part([TAPS * HEADS])
        st_c = part([OWN, 6])
        mv_c = part([OWN, 2])
        arg_c = part([OWN])
        rstd_c = part([OWN])
        shift_c = part([OWN])
        y_cur = [part([C]) for q in range(2)]
        yT_cur = [part([P]) for q in range(2)]
        mx = [part([HEADS]) for q in range(2)]
        logit = [part([TAPS * HEADS]) for q in range(2)]
        e_w = [part([TAPS * HEADS]) for q in range(2)]
        esum = [part([HEADS]) for q in range(2)]
        erec = [part([HEADS]) for q in range(2)]
        avg = [part([C]) for q in range(2)]

        st = [sb(f"st{q}", [P, NT, 6]) for q in range(2)]
        mv = [sb(f"mv{q}", [P, NT, 2]) for q in range(2)]
        arg = [sb(f"arg{q}", [P, 3, NT]) for q in range(2)]
        expo = sb("expo", [P, 3, NT])
        rstd = [sb(f"rstd{q}", [P, 3, NT]) for q in range(2)]
        z = [sb(f"z{q}", [P, NT, C]) for q in range(2)]

        cursor[0] = 0
        xnT = part([B * T])
        gam_beta = sb("gam_beta", [P, 2])
        w_q = sb("w_q", [P, C])
        w_raw = sb("w_raw", [P, C])
        w_scr = sb("w_scr", [P, C])
        w_beta = sb("w_beta", [P, 4])
        ones = sb("ones", [P, P])
        amax = sb("amax", [P, B])
        amax1 = sb("amax1", [P, 1])
        gmax = sb("gmax", [P, 1])
        bound = sb("bound", [P, 2])
        clipped = [part([T]) for q in range(2)]
        feed_forward_end = cursor[0]

        dft_f = sb("dft_f", [P, 2, 6 * P])
        dft_i = sb("dft_i", [P, 4, WIN])
        sgn = sb("sgn", [P, 1])
        t_in = sb("t_in", [P, NT, C])
        kf = [sb(f"kf{j}", [P, 3, 2, C]) for j in range(2)]
        xi_sb = None
        cursor[0] = 0
        qT = [part([PAIRS, T], BF16) for q in range(2)]
        probs = [part([4, 1024]) for q in range(2)]
        zeroed = cursor[0]
        kT = [part([PAIRS, NJ, 2 * KB], BF16) for q in range(2)]
        split_q = part([NT * HEADS, ROWS_B], BF16)
        split_k = part([NT * HEADS, ROWS_B], BF16)
        v_pair = [part([NJ, PAIRS, 32]) for q in range(2)]
        zeroed = slice(zeroed, cursor[0])
        assert zeroed.start >= feed_forward_end
        coord = part([2, 2 * NT * HEADS, 6])
        m_a = part([2, NT * HEADS, COMPS])
        m_b = part([2, NT * HEADS, COMPS])
        line = part([2, NT * HEADS, COMPS])
        rest = part([2, NT * HEADS, COMPS])
        len2 = part([2 * NT * HEADS])
        inv_len = part([2 * NT * HEADS])
        guess = part([2 * NT * HEADS])
        newton = part([2 * NT * HEADS])
        probs_c2 = part([4, 256])
        pv_sb = part([T])
        inv_den = part([NT, 8])
        att = part([NT, C])
        attT = part([T])
        w_qk = sb("w_qk", [P, 2, C])
        w_qp = sb("w_qp", [P, 2, C // 2])
        w_val = sb("w_val", [P, C])
        w_o = sb("w_o", [P, C])
        b_v = sb("b_v", [P, 1])
        b_v_wide = sb("b_v_wide", [P, P])
        ones_row = sb("ones_row", [1, P])
        b_o_row = sb("b_o_row", [1, C])
        att_bias = sb("att_bias", [P, C])
        mask = sb("mask", [P, KB])

        cursor[0] = 0
        pr = [part([2, 2, C]) for n in range(4)]
        pu = [part([2, C]) for n in range(4)]
        yf = [part([2, 2, 2, C]) for q in range(2)]

        w_r = sb("w_r", [P, C])
        w_k = sb("w_k", [P, C])
        w_v = sb("w_v", [P, C])
        mus = sb("mus", [P, 2])
        zT = [sb(f"zT{q}", [P, 1 + T]) for q in range(2)]
        cursor[0] = 0
        dif = [part([T]) for q in range(2)]
        xrT = [part([T]) for q in range(2)]
        xkT = [part([T]) for q in range(2)]
        kact = [part([T]) for q in range(2)]
        rsig = [part([NT * C]) for q in range(2)]
        gated = [part([NT * C]) for q in range(2)]

        w_in = sb("w_in", [P, INNER])
        w_gate = sb("w_gate", [P, INNER])
        w_b = sb("w_b", [P, MI, INNER])
        w_c = sb("w_c", [P, MI, INNER])
        w_d = sb("w_d", [P, MI, INNER])
        w_out = sb("w_out", [P, MI, C])
        w_od = sb("w_od", [P, MI, C])
        vecs = sb("vecs", [P, 6, MI])
        norm_w = sb("norm_w", [P, 1])
        decay = sb("decay", [P, MI])
        decay_row = part([MI, T])
        out_b_row = sb("out_b_row", [1, C])
        bias_row = sb("bias_row", [P, C])
        x_plus = [part([NT * C]) for q in range(2)]
        gate = [part([T]) for m in range(MI)]
        uT = [part([MI, T]) for q in range(2)]
        bT = [part([T]) for m in range(MI)]
        hT = [part([T]) for m in range(MI)]
        chT = [part([MI, T]) for q in range(2)]
        x_dram = nc.dram_tensor("x_after_conv", (B * T, C), F32).ap()

        S = {}

        def s(name):
            if name not in S:
                S[name] = sem(name)
            return S[name]

        CARRY = {}
        COLUMNS = []

        def at(e, name, count):
            e.wait_ge(s(name), count)
            if not isinstance(count, int):
                if id(e) not in CARRY:
                    CARRY[id(e)] = e.alloc_register(f"carry{len(CARRY)}")
                if e is nc.scalar:
                    e.reg_mov(CARRY[id(e)], 0)
                else:
                    e.reg_alu(CARRY[id(e)], count, 1, ALU.add)

        def column(e, value, most):
            if isinstance(value, int):
                return value
            reg = e.alloc_register(f"column{len(COLUMNS)}")
            COLUMNS.append(reg)
            e.reg_mov(reg, value)
            return e.snap(reg, min_val=0, max_val=most)

        def pairs(e, body, ahead=False, behind=False, count=B):
            apart = 2 * ahead
            if behind:
                body(0, 0)
                body(1, 1)
            with e.Fori(2 if behind else 0, count - apart - 1, 2) as b:
                body(b, 0)
                body(b + 1, 1)
            for b in range(count - apart, count):
                body(b, b % 2)

        def inside(n, count=OWN):
            return not isinstance(n, int) or 0 <= n < count

        def tok(b, n=NT):
            if isinstance(b, int):
                return slice(b * T, b * T + T)
            return bass.ds(b * T, T)

        def tile(b, i):
            if isinstance(b, int):
                return slice((b * NT + i) * C, (b * NT + i + 1) * C)
            return bass.ds(b * T + i * C, C)

        def vtok(b, k):
            return slice(k, k + 1)

        ln_stages = [x for x in STAGES if x != "conv" and x in stages]
        turn_stages = [x for x in ln_stages if x != "toep"]
        upd = {x: n for n, x in enumerate(ln_stages)}
        turn = {x: n for n, x in enumerate(turn_stages)}

        def ln_stats(e, stage, b, q, fac, add, extra=False):
            n = B * upd[stage] + b
            if upd[stage] == 0:
                at(e, "x_loaded", 16 * b + 16)
            else:
                at(e, "x_updated", n - B + B * 0 + 1)
            for i in range(NT):
                e.bn_stats(st[q][:, i, :], x_tile[:, tile(b, i)])
            e.drain()
            for i in range(NT):
                e.bn_aggr(mv[q][:, i, :], st[q][:, i, :])
            e.drain()
            ins = e.tensor_scalar(arg[q][:, 0, :], mv[q][:, :, 1], fac, add, ALU.mult, ALU.add)
            if extra:
                e.tensor_scalar(arg[q][:, 1, :], mv[q][:, :, 1], fac, add, ALU.mult, ALU.add)
                ins = e.tensor_scalar(arg[q][:, 2, :], mv[q][:, :, 1], LN_EPS, None, ALU.add)
            ins.then_inc(s("var_ready"), 1)

        def ln_rstd(e, stage, b, q, k=1):
            n = B * upd[stage] + b
            e.wait_ge(s("var_ready"), n + 1)
            e.tensor_tensor(rstd[q][:, 0:k, :], arg[q][:, 0:k, :], expo[:, 0:k, :], ALU.pow).then_inc(s("rstd_ready"), 1)

        def ln_norm(e, stage, b, q):
            n = B * upd[stage] + b
            e.wait_ge(s("rstd_ready"), n + 1)
            if not (isinstance(b, int) and b < 2):
                if stage == "toep":
                    at(e, "toep_z_used", b - 1)
                else:
                    at(e, "turned", B * turn[stage] + b - 1)
            for i in range(NT):
                ins = e.tensor_scalar(z[q][:, i, :], x_tile[:, tile(b, i)], mv[q][:, i, 0:1], rstd[q][:, 0, i:i + 1],
                                      ALU.subtract, ALU.mult)
            ins.then_inc(s("z_ready"), 1)

        def turn_z(e, stage, b, q):
            e.wait_ge(s("z_ready"), B * upd[stage] + b + 1)
            e.wait_ge(s("turn_bank_free"), B * turn[stage] + b + 1)
            for i in range(NT):
                ins = e.transpose(bank(6 + q)[:, P * i:P * i + P], z[q][:, i, :], ident[:, :])
            ins.then_inc(s("turned"), 1)

        LN_CONST = {"ffn": (1 + D_FFN_EPS, LN_EPS * D_FFN_EPS), "plain": (1.0, LN_EPS),
                    "scan": (1 + NORM_EPS, LN_EPS * NORM_EPS)}
        kind = {"ffn0": "ffn", "ffn1": "ffn", "attn": "plain", "toep": "plain", "mix0": "plain", "mix1": "plain",
                "scan": "scan"}
        N_LOAD = 27 if "conv" in stages else 28
        BLOCK_CHUNKS = [(c, c + OWN // 4) for c in range(0, OWN, OWN // 4)]
        block = ctx.enter_context(nc.Block())

        def stage_gate(e, stage):
            if upd[stage] > 0:
                e.wait_ge(s("x_updated"), B * upd[stage])

        @block.sync
        def _(e):
            if "conv" in stages:
                for c, (lo, hi) in enumerate(BLOCK_CHUNKS):
                    e.dma_start(x_blk[:, lo * C:hi * C], d["x"][:, lo * C:hi * C]).then_inc(s(f"x_blk{c}"), 16)
                e.dma_start(w_conv[:, :], d["w_lin"]).then_inc(s("conv_w"), 16)
                e.dma_start(ident[:, :], d["ident"]).then_inc(s("conv_w"), 16)
            else:
                e.dma_start(ident[:, :], d["ident"]).then_inc(s("weights"), 16)
            loads = [(gam_beta[:, :], d["gam_beta"]),
                     (w_raw[:, :], d["weight"]), (dft_f[:, :, :], d["dft_f"]), (dft_i[:, :, :], d["dft_i"]),
                     (sgn[:, :], d["sgn"]), (t_in[:, :, :], d["t"]), (w_r[:, :], d["W_r"]), (w_k[:, :], d["W_k"]),
                     (w_v[:, :], d["W_v"]), (mus[:, :], d["mus"]), (w_in[:, :], d["in_w"]), (w_gate[:, :], d["gate_w"]),
                     (w_b[:, :, :], d["b_w"]), (w_c[:, :, :], d["c_w"]), (w_d[:, :, :], d["d_w"]),
                     (w_out[:, :, :], d["out_w"]), (vecs[:, :, :], d["vecs"]), (norm_w[:, :], d["norm_w"]),
                     (out_b_row[:, :], d["out_b"]), (expo[:, :, :], d["expo"]), 
                     (w_qk[:, :, :], d["w_qk"]), (w_qp[:, :, :], d["w_qp"]), (w_val[:, :], d["w_val"]), (w_o[:, :], d["W_o"]),
                     (b_v[:, :], d["b_v"]), (b_o_row[:, :], d["b_o"]), (mask[:, :], d["mask"])]
            assert len(loads) == N_LOAD - (0 if "conv" in stages else 1)
            for dst, src in loads:
                e.dma_start(dst, src).then_inc(s("weights"), 16)
            if "conv" in stages:
                e.wait_ge(s("conv_y"), 2)
                e.wait_ge(s("halo_zero"), 1)
                for b in range(B):
                    lo = b * PER_SEQ
                    e.dma_start(y_ext[lo + 1:lo + PER_SEQ, 0:REACH * C],
                                y_ext[lo:lo + PER_SEQ - 1, OWN * C:(OWN + REACH) * C]).then_inc(s("halo"), 16)
                xd = x_dram.rearrange("(p t) c -> p (t c)", t=OWN)
                for n in range(0, OWN, OWN // 8):
                    cols = slice((OWN - n - OWN // 8) * C, (OWN - n) * C)
                    e.wait_ge(s("conv_x"), n + OWN // 8)
                    e.dma_start(xd[:, cols], x_blk[:, cols]).then_inc(s("x_stored"), 16)
                e.wait_ge(s("x_stored"), 16 * 8)
            src = (x_dram if "conv" in stages else d["x"].rearrange("p (t c) -> (p t) c", c=C))
            src = src.rearrange("(n p) c -> p n c", p=P)
            for b in range(B):
                e.dma_start(x_tile[:, b * T:(b + 1) * T].rearrange("p (n c) -> p n c", c=C),
                            src[:, b * NT:(b + 1) * NT, :]).then_inc(s("x_loaded"), 16)
                e.wait_ge(s("x_loaded"), 16 * b + 16)
            od = out.rearrange("(n p) c -> p n c", p=P)
            for b in range(B):
                if ln_stages:
                    e.wait_ge(s("x_updated"), B * (len(ln_stages) - 1) + b + 1)
                e.dma_start(od[:, b * NT:(b + 1) * NT, :],
                            x_tile[:, b * T:(b + 1) * T].rearrange("p (n c) -> p n c", c=C)).then_inc(s("out_stored"), 16)
            e.wait_ge(s("out_stored"), 16 * B)

        def own(n, buf_off=0):
            return bass.ds((OWN - 1) * C - n * C + buf_off, C)

        def window(n, k0, k1):
            return bass.ds((OWN - 1 + k0) * C - n * C, (k1 - k0) * C)

        @block.gpsimd
        def _(e):
            e.memset(minus_half[:, :], -0.5)
            e.drain()
            e.memset(ones[:, :], 1.0 / (P * C)).then_inc(s("ones"), 1)
            for q in range(2):
                e.memset(zT[q][:, 0:1], 0.0).then_inc(s("zT_zero"), 1)
            if "conv" in stages:
                e.memset(y_ext[:, 0:REACH * C], 0.0).then_inc(s("halo_zero"), 1)
                for h in range(2):
                    some = slice(h * OWN // 2, (h + 1) * OWN // 2)
                    e.wait_ge(s("conv_var"), h + 1)
                    e.tensor_tensor(rstd_c[:, some], arg_c[:, some], minus_half[:, some], ALU.pow).then_inc(s("conv_rstd"), 1)
                e.wait_ge(s("conv_y"), 2)
                e.wait_ge(s("halo"), 16 * B)

                def taps(n, q):
                    k0 = DVE_TAPS
                    first = column(e, (OWN - 1 + k0) * C - n * C, (OWN - 1 + k0) * C)
                    first_rest = column(e, (OWN - 1 + k0 + PRE_ADDED) * C - n * C, (OWN - 1 + k0 + PRE_ADDED) * C)
                    e.wait_ge(s("conv_e"), n + 1)
                    at(e, "prod_free", n + 1)
                    for k, col, m in ((k0, first, PRE_ADDED), (k0 + PRE_ADDED, first_rest, TAPS - k0 - PRE_ADDED)):
                        e.tensor_tensor(prod[q][:, k * C:(k + m) * C].rearrange("p (k h r) -> p k h r", h=HEADS, r=R),
                                        y_ext[:, bass.ds(col, m * C)].rearrange("p (k h r) -> p k h r", h=HEADS, r=R),
                                        e_w[q][:, k * HEADS:(k + m) * HEADS].rearrange("p (k h) -> p k h", h=HEADS).unsqueeze(3)
                                        .to_broadcast([P, m, HEADS, R]), ALU.mult).then_inc(s("prod_pool"), 1)

                def add_x(n, q):
                    first = column(e, (OWN - 1) * C - n * C, (OWN - 1) * C)
                    at(e, "conv_avg", n + 1)
                    e.tensor_tensor(x_blk[:, bass.ds(first, C)], x_blk[:, bass.ds(first, C)], avg[q][:, :], ALU.add).then_inc(s("conv_x"), 1)

                taps(0, 0)

                def body(n, q):
                    if inside(n + 1):
                        taps(n + 1, 1 - q)
                    if inside(n - 1):
                        add_x(n - 1, 1 - q)
                pairs(e, body, ahead=1, behind=True, count=OWN)
                add_x(OWN - 1, 1)
            e.wait_ge(s("weights"), 16 * N_LOAD)

            for stage in ln_stages:
                k = 3 if stage == "scan" else 1
                if stage == "ffn0" or stage == "ffn1":
                    middle = (zeroed.start + zeroed.stop) // 2
                    if stage == "ffn0":
                        e.memset(shared[:, zeroed.start:middle], 0.0)
                    pairs(e, lambda b, q: ln_rstd(e, stage, b, q))
                    if stage == "ffn0":
                        e.memset(shared[:, middle:zeroed.stop], 0.0)
                        e.memset(ones_row[:, :], 1.0)
                        e.drain()
                        for q in range(2):
                            e.memset(v_pair[q][0:KB, :, :, D_HEAD:D_HEAD + 1], 1.0)
                            e.memset(v_pair[q][KB:P, :, :, 16 + D_HEAD:17 + D_HEAD], 1.0)
                        e.drain().then_inc(s("attn_init"), 1)
                    e.wait_ge(s("amax"), 1 if stage == "ffn0" else 2)
                    e.partition_all_reduce(gmax[:, :], amax1[:, :], P, bass.bass_isa.ReduceOp.max).then_inc(s("gmax"), 1)
                elif stage == "attn":
                    stage_gate(e, stage)
                    e.wait_ge(s("att_bias"), 1)

                    def lengths(b, q):
                        e.wait_ge(s("len_guess"), b + 1)
                        e.tensor_tensor(newton[:, :], guess[:, :], guess[:, :], ALU.mult)
                        e.drain()
                        e.tensor_tensor(newton[:, :], newton[:, :], len2[:, :], ALU.mult)
                        e.drain()
                        e.tensor_scalar(newton[:, :], newton[:, :], -0.5 * 8.0 ** ROOT_SHIFT, 1.5 * 2.0 ** ROOT_SHIFT, ALU.mult, ALU.add)
                        e.drain()
                        e.tensor_tensor(inv_len[:, :], guess[:, :], newton[:, :], ALU.mult).then_inc(s("inv_len"), 1)

                    def add_bias(b, q):
                        first = column(e, b * T, (B - 1) * T)
                        at(e, "z_ready", B * upd[stage] + b + 1)
                        xv = x_tile[:, bass.ds(first, T)] if not isinstance(first, int) else x_tile[:, first:first + T]
                        xv = xv.rearrange("p (i c) -> p i c", c=C)
                        e.tensor_tensor(xv, xv, att_bias[:, :].unsqueeze(1).to_broadcast([P, NT, C]), ALU.add).then_inc(s("x_biased"), 1)

                    def masks(b, k):
                        c = k % 3
                        e.wait_ge(s("p_ready"), UNITS * b + 9 * (k // 3) + (4, 8, 9)[c])
                        for j, col in CHUNK_BLOCKS[c]:
                            pv = probs_c2[:, :, 0:KB] if c == 2 else probs[c][:, :, col:col + KB]
                            ins = e.tensor_tensor(pv, pv, mask[:, :].unsqueeze(1).to_broadcast([P, 4, KB]), ALU.mult)
                        ins.then_inc(s("masked"), 1)

                    ln_rstd(e, stage, 0, 0)
                    lengths(0, 0)
                    add_bias(0, 0)
                    ln_rstd(e, stage, 1, 1)

                    def body(b, q):
                        last = isinstance(b, int) and b == B - 1
                        if not last:
                            add_bias(b + 1, 1 - q)
                        masks(b, 0)
                        masks(b, 1)
                        masks(b, 2)
                        if not (isinstance(b, int) and b >= B - 2):
                            ln_rstd(e, stage, b + 2, q)
                        if not last:
                            lengths(b + 1, 1 - q)
                        for k in range(3, CHUNKS):
                            masks(b, k)
                    pairs(e, body, ahead=True)
                elif stage == "toep":
                    def body(b, q):
                        ln_rstd(e, stage, b, q)
                        e.wait_ge(s("toep_pu"), b + 1)
                        e.tensor_tensor(pu[0][:, :, :], pu[0][:, :, :], pu[1][:, :, :], ALU.subtract)
                        e.tensor_tensor(pu[2][:, :, :], pu[2][:, :, :], pu[3][:, :, :], ALU.add).then_inc(s("toep_cross"), 1)
                    pairs(e, body)
                elif stage in ("mix0", "mix1"):
                    mb = 0 if stage == "mix0" else B

                    ln_rstd(e, stage, 0, 0)
                    ln_rstd(e, stage, 1, 1)

                    def body(b, q):
                        if inside(b + 2, B):
                            ln_rstd(e, stage, b + 2, q)
                        at(e, "mix_gated", mb + b + 1)
                        e.tensor_tensor(x_tile[:, tok(b)], x_tile[:, tok(b)], gated[q][:, :], ALU.add).then_inc(s("x_updated"), 1)
                    pairs(e, body, ahead=True)
                elif stage == "scan":
                    def ratio(b, q):
                        e.wait_ge(s("rstd_ready"), B * upd[stage] + b + 1)
                        e.tensor_tensor(rstd[q][:, 1, :], rstd[q][:, 1, :], rstd[q][:, 2, :], ALU.mult).then_inc(s("ratio"), 1)

                    ln_rstd(e, stage, 0, 0, 3)
                    ratio(0, 0)
                    ln_rstd(e, stage, 1, 1, 3)

                    def body(b, q):
                        if inside(b + 1, B):
                            ratio(b + 1, 1 - q)
                        if inside(b + 2, B):
                            ln_rstd(e, stage, b + 2, q, 3)
                    pairs(e, body, ahead=True)
                else:
                    pairs(e, lambda b, q: ln_rstd(e, stage, b, q))

        @block.tensor
        def _(e):
            if "conv" in stages:
                e.wait_ge(s("conv_w"), 32)

                def turn_y(n, q):
                    e.wait_ge(s("y_cur"), n + 1)
                    if inside(n - 2):
                        e.wait_ge(s("yT_cur"), n - 1)
                    e.transpose(bank(q)[:, 0:P], y_cur[q][:, :], ident[:, :]).then_inc(s("yT_bank"), 1)

                def logits(n, q):
                    e.wait_ge(s("yT_cur"), n + 1)
                    if inside(n - 2):
                        e.wait_ge(s("conv_e"), n - 1)
                    e.matmul(bank(2 + q)[:, 0:TAPS * HEADS], yT_cur[q][:, :], w_conv[:, :], start=True, stop=True) \
                        .then_inc(s("logits"), 1)

                def total(n, q):
                    if inside(n - 2):
                        e.wait_ge(s("conv_avg"), n - 1)
                    e.wait_ge(s("prod_vec"), n + 1)
                    e.wait_ge(s("prod_pool"), 2 * n + 2)
                    kept = [k for k in range(TAPS) if not DVE_TAPS <= k < DVE_TAPS + PRE_ADDED]
                    for k in kept:
                        ins = e.matmul(bank(4 + q)[:, 0:C], ident[:, :], prod[q][:, k * C:k * C + C], start=(k == kept[0]),
                                       stop=(k == kept[-1]))
                    ins.then_inc(s("prod_free"), 1)

                turn_y(0, 0)
                turn_y(1, 1)
                logits(0, 0)
                turn_y(2, 0)
                logits(1, 1)
                turn_y(3, 1)
                logits(2, 0)

                def body(n, q):
                    if inside(n + 3):
                        logits(n + 3, 1 - q)
                    if inside(n + 4):
                        turn_y(n + 4, q)
                    total(n, q)
                pairs(e, body, ahead=3, behind=True, count=OWN)

            e.wait_ge(s("weights"), 16 * N_LOAD)
            if "ffn0" in stages:
                e.wait_ge(s("w_abs"), 1)
                e.wait_ge(s("ones"), 1)
                e.matmul(bank(5)[:, 0:1], ones[:, :], w_beta[:, 0:1], start=True, stop=True).then_inc(s("w_mean"), 1)

            for stage in ln_stages:
                if stage in ("ffn0", "ffn1"):
                    fb = 0 if stage == "ffn0" else B
                    stage_gate(e, stage)
                    pairs(e, lambda b, q: turn_z(e, stage, b, q))

                    def body(b, q):
                        e.wait_ge(s("clipped"), fb + b + 1)
                        for i in range(NT):
                            ins = e.matmul(bank(q)[:, C * i:C * i + C], clipped[q][:, P * i:P * i + P], w_q[:, :],
                                           start=True, stop=True)
                        ins.then_inc(s("ffn_y"), 1)
                    pairs(e, body)
                elif stage == "attn":
                    stage_gate(e, stage)
                    e.wait_ge(s("attn_init"), 1)
                    e.wait_ge(s("b_v_wide"), 1)
                    e.matmul(bank(4)[:, 0:C], b_v_wide[:, :], w_o[:, :], start=True, stop=False)
                    e.matmul(bank(4)[:, 0:C], ones_row[:, :], b_o_row[:, :], start=False, stop=True).then_inc(s("bias_bank"), 1)
                    nt = B * turn[stage]

                    def turn5(b, q):
                        e.wait_ge(s("z_ready"), B * upd[stage] + b + 1)
                        if not (isinstance(b, int) and b == 0):
                            e.wait_ge(s("v_copied"), 2 * b)
                        for i in range(NT):
                            ins = e.transpose(bank(5)[:, P * i:P * i + P], z[q][:, i, :], ident[:, :])
                        ins.then_inc(s("turned"), 1)

                    def project(b, q, v):
                        if v == 0:
                            e.wait_ge(s("turn_bank_free"), nt + b + 3)
                        else:
                            e.wait_ge(s("coord_copied"), 2 * b + 1)
                        for i in range(NT):
                            dst = bank(5)[:, C * i:C * i + C]
                            e.matmul(dst, zT[q][:, 1 + P * i:1 + P * i + P], w_qk[:, v, :], start=True, stop=False)
                            ins = e.matmul(dst[:, 0:C // 2], zT[q][:, P * i:P * i + P], w_qp[:, v, :], start=False, stop=True)
                        ins.then_inc(s("coord_bank"), 1)

                    def value_rows(b, q):
                        e.wait_ge(s("coord_copied"), 2 * b + 2)
                        for j in range(NJ):
                            toks = zT[q][:, 1 + KB * j:1 + KB * j + KB]
                            e.matmul(bank(5)[0:KB, KB * j:KB * j + KB], toks, w_val[:, 0:KB], start=True, stop=True)
                            ins = e.matmul(bank(5)[KB:P, KB * j:KB * j + KB], toks, w_val[:, KB:2 * KB], start=True, stop=True)
                        ins.then_inc(s("v_bank"), 1)

                    def turn_qk(b, q, r):
                        e.wait_ge(s("split"), 2 * b + 2)
                        if not (isinstance(b, int) and b == 0 and r == 0):
                            e.wait_ge(s("qk_copied"), PAIRS * b + r)
                        for side, src in enumerate((split_q, split_k)):
                            dst = bank(7).bitcast(BF16)[0:QK_ROWS, T * side:T * side + T]
                            for i in range(NT):
                                rows = src[:, HEADS * i + 2 * r:HEADS * i + 2 * r + 2, :].rearrange("p h r -> p (h r)")
                                ins = e.transpose(dst[:, P * i:P * i + P], rows[:, 0:QK_ROWS], ident_b[:, :])
                        ins.then_inc(s("qk_turned"), 1)

                    def scores(b, q, u):
                        g, c, i0 = u // 9, min(u % 9 // 4, 2), u % 9 % 4
                        if c == 0 or c == 2:
                            last_pair = 4 * g + (3 if c == 2 else i0)
                            e.wait_ge(s("qk_copied"), PAIRS * b + last_pair + 1)
                        if not (isinstance(b, int) and b == 0 and u < 2):
                            e.wait_ge(s("p_ready"), UNITS * b + u - 1)
                        for i in (range(4) if c == 2 else (i0,)):
                            p = 4 * g + i
                            for j, col in CHUNK_BLOCKS[c]:
                                col += 256 * i if c == 2 else 0
                                ins = e.matmul(bank(2 * (u % 2), 2)[:, col:col + T - KB * j], kT[q][0:QK_ROWS, p, j, :],
                                               qT[q][0:QK_ROWS, p, KB * j:T], start=True, stop=True)
                        ins.then_inc(s("scored"), 1)

                    def weigh(b, q, k, half=None):
                        g, c = k // 3, k % 3
                        if half != 1:
                            e.wait_ge(s("masked"), CHUNKS * b + k + 1)
                            if k == 0:
                                e.wait_ge(s("v_copied"), 2 * b + 2)
                            if c == 0 and not (isinstance(b, int) and b == 0 and g == 0):
                                e.wait_ge(s("pv_copied"), 2 * b + g)
                        blocks = CHUNK_BLOCKS[c]
                        cut = 1 if c == 0 else 2
                        if half is not None:
                            blocks = blocks[:cut] if half == 0 else blocks[cut:]
                        for j, col in blocks:
                            for i in range(4):
                                pr_ = probs_c2[:, i, :] if c == 2 else probs[c][:, i, col:col + T - KB * j]
                                ins = e.matmul(bank(4)[32 * i:32 * i + 32, KB * j:T], v_pair[q][:, j, 4 * g + i, :], pr_,
                                               start=(j == 0), stop=(j == 4))
                        if half != 0:
                            ins.then_inc(s("weighed"), 1)

                    def turn_pv(b, g):
                        e.wait_ge(s("pv_copied"), 2 * b + g + 1)
                        for i in range(NT):
                            ins = e.transpose(bank(6)[:, P * i:P * i + P], pv_sb[:, P * i:P * i + P], ident[:, :])
                        ins.then_inc(s("pv_turned"), 1)

                    def turn_att(b):
                        e.wait_ge(s("att_ready"), 2 * b + 2)
                        for i in range(NT):
                            ins = e.transpose(bank(6)[:, P * i:P * i + P], att[:, i, :], ident[:, :])
                        ins.then_inc(s("att_turned"), 1)

                    def out_rows(b):
                        e.wait_ge(s("aT_copied"), b + 1)
                        for i in range(NT):
                            ins = e.matmul(bank(6)[:, C * i:C * i + C], attT[:, P * i:P * i + P], w_o[:, :], start=True, stop=True)
                        ins.then_inc(s("att_out"), 1)

                    turn5(0, 0)
                    project(0, 0, 0)
                    project(0, 0, 1)
                    value_rows(0, 0)
                    turn_qk(0, 0, 0)
                    turn_qk(0, 0, 1)

                    def body(b, q):
                        first, last = (isinstance(b, int) and b == x for x in (0, B - 1))
                        scores(b, q, 0)
                        turn_qk(b, q, 2)
                        scores(b, q, 1)
                        turn_qk(b, q, 3)
                        if not first:
                            weigh(b - 1, 1 - q, 4, 0)
                        if not last:
                            turn5(b + 1, 1 - q)
                        scores(b, q, 2)
                        if not first:
                            weigh(b - 1, 1 - q, 4, 1)
                        turn_qk(b, q, 4)
                        scores(b, q, 3)
                        if not first:
                            weigh(b - 1, 1 - q, 5)
                        turn_qk(b, q, 5)
                        if not last:
                            project(b + 1, 1 - q, 0)
                        scores(b, q, 4)
                        if not first:
                            turn_pv(b - 1, 1)
                        turn_qk(b, q, 6)
                        scores(b, q, 5)
                        if not last:
                            project(b + 1, 1 - q, 1)
                        turn_qk(b, q, 7)
                        scores(b, q, 6)
                        if not first:
                            turn_att(b - 1)
                        weigh(b, q, 0, 0)
                        scores(b, q, 7)
                        if not last:
                            value_rows(b + 1, 1 - q)
                        weigh(b, q, 0, 1)
                        scores(b, q, 8)
                        if not first:
                            out_rows(b - 1)
                        scores(b, q, 9)
                        weigh(b, q, 1, 0)
                        scores(b, q, 10)
                        weigh(b, q, 1, 1)
                        scores(b, q, 11)
                        weigh(b, q, 2)
                        scores(b, q, 12)
                        scores(b, q, 13)
                        turn_pv(b, 0)
                        scores(b, q, 14)
                        weigh(b, q, 3, 0)
                        scores(b, q, 15)
                        weigh(b, q, 3, 1)
                        for u in (16, 17):
                            scores(b, q, u)
                            if not last:
                                turn_qk(b + 1, 1 - q, u - 16)
                    pairs(e, body, ahead=True, behind=True)
                    weigh(B - 1, 1, 4)
                    weigh(B - 1, 1, 5)
                    turn_pv(B - 1, 1)
                    turn_att(B - 1)
                    out_rows(B - 1)
                elif stage == "toep":
                    stage_gate(e, stage)
                    for v, m0 in enumerate((0, 4, 5)):
                        for h in range(2):
                            m = {0: (0, 1), 4: (4, 3), 5: (5, 1)}[m0][h]
                            dst = bank(v)[:, 256 * h:256 * h + 256].rearrange("p (w c) -> p w c", w=2)
                            for k in range(2):
                                ins = e.matmul(dst, dft_f[:, k, P * m:P * m + P], t_in[:, k:NT:2, :], start=(k == 0), stop=(k == 1))
                    ins.then_inc(s("kernel_bank"), 1)
                    e.wait_ge(s("kernel_ready"), 1)

                    def forward(b, q):
                        e.wait_ge(s("z_ready"), B * upd[stage] + b + 1)
                        e.wait_ge(s("toep_bank_free"), b + 1)
                        for m in range(4):
                            dst = bank(2 * q, 2)[:, 256 * m:256 * m + 256].rearrange("p (w c) -> p w c", w=2)
                            for k in range(2):
                                ins = e.matmul(dst, dft_f[:, k, P * m:P * m + P], z[q][:, k:NT:2, :], start=(k == 0), stop=(k == 1))
                        ins.then_inc(s("toep_z_used"), 1)

                    def inverse(b, q):
                        e.wait_ge(s("toep_spec"), b + 1)
                        for k in range(2):
                            dst = bank(4 + q)[:, 256 * k:256 * k + 256]
                            for m in range(4):
                                ins = e.matmul(dst, dft_i[:, m, P * k:P * k + P],
                                               yf[q][:, m // 2, m % 2, :, :].rearrange("p w c -> p (w c)"),
                                               start=(m == 0), stop=(m == 3))
                        ins.then_inc(s("toep_out"), 1)
                    forward(0, 0)

                    def body(b, q):
                        if not (isinstance(b, int) and b == B - 1):
                            forward(b + 1, 1 - q)
                        inverse(b, q)
                    pairs(e, body, ahead=True)
                elif stage in ("mix0", "mix1"):
                    mb = 0 if stage == "mix0" else B
                    stage_gate(e, stage)

                    def keys(b, q):
                        e.wait_ge(s("mix_xk"), mb + b + 1)
                        e.wait_ge(s("mix_k_free"), mb + b + 1)
                        e.matmul(bank(q), w_k[:, :], xkT[q][:, :], start=True, stop=True).then_inc(s("mix_k"), 1)
                        e.wait_ge(s("mix_r_free"), mb + b + 1)
                        for i in range(NT):
                            ins = e.matmul(bank(2 + q)[:, C * i:C * i + C], xrT[q][:, P * i:P * i + P], w_r[:, :], start=True, stop=True)
                        ins.then_inc(s("mix_r"), 1)

                    def values(b, q):
                        e.wait_ge(s("mix_kact"), mb + b + 1)
                        if not (isinstance(b, int) and b < 2):
                            e.wait_ge(s("mix_gated"), mb + b - 1)
                        for i in range(NT):
                            ins = e.matmul(bank(4 + q)[:, C * i:C * i + C], kact[q][:, P * i:P * i + P], w_v[:, :], start=True, stop=True)
                        ins.then_inc(s("mix_v"), 1)
                    turn_z(e, stage, 0, 0)
                    turn_z(e, stage, 1, 1)
                    keys(0, 0)

                    def body(b, q):
                        values(b, q)
                        if inside(b + 1, B):
                            keys(b + 1, 1 - q)
                        if inside(b + 2, B):
                            turn_z(e, stage, b + 2, q)
                    pairs(e, body, ahead=True, behind=True)
                elif stage == "scan":
                    stage_gate(e, stage)
                    e.wait_ge(s("scan_const"), 1)
                    for m in range(MI):
                        for j in range(MI):
                            e.matmul(bank(5)[:, C * m:C * m + C], w_d[:, j, P * m:P * m + P], w_out[:, j, :],
                                     start=(j == 0), stop=(j == MI - 1))
                    for j in range(MI):
                        e.matmul(bank(4)[:, 0:C], decay_row[:, j, 0:P], w_out[:, j, :], start=(j == 0), stop=False)
                    e.matmul(bank(4)[:, 0:C], decay_row[0:1, 0, P:2 * P], out_b_row[:, :], start=False, stop=True) \
                        .then_inc(s("scan_fold"), 1)
                    e.wait_ge(s("scan_ready"), 1)

                    def gates(b, q):
                        e.wait_ge(s("turn_bank_free"), B * turn[stage] + b + 3)
                        for m in range(MI):
                            if not (isinstance(b, int) and b < 1):
                                e.wait_ge(s("u_ready"), MI * (b - 1) + m + 1)
                            e.matmul(bank(2 * m), w_in[:, P * m:P * m + P], xrT[q][:, :], start=True, stop=True)
                            e.matmul(bank(2 * m + 1), w_gate[:, P * m:P * m + P], xrT[q][:, :], start=True, stop=True) \
                                .then_inc(s("ug"), 1)

                    def states(b, q):
                        e.wait_ge(s("u_ready"), MI * b + MI)
                        for m in range(MI):
                            e.wait_ge(s("b_free"), MI * b + m + 1)
                            for j in range(MI):
                                ins = e.matmul(bank(4), w_b[:, j, P * m:P * m + P], uT[q][:, j, :], start=(j == 0), stop=(j == MI - 1))
                            ins.then_inc(s("b_bank"), 1)
                            if not (isinstance(b, int) and b == 0 and m == 0):
                                e.wait_ge(s("ch_ready"), MI * b + m)
                            for j in range(MI):
                                ins = e.matmul(bank(5), w_c[:, j, P * m:P * m + P], uT[q][:, j, :], start=(j == 0), stop=(j == MI - 1))
                            ins.then_inc(s("c_bank"), 1)

                    def outs(b, q):
                        e.wait_ge(s("ch_ready"), MI * b + MI)
                        e.wait_ge(s("x_updated"), B * upd[stage] + b)
                        for i in range(NT):
                            for j in range(MI):
                                e.matmul(bank(7)[:, C * i:C * i + C], uT[q][:, j, P * i:P * i + P], w_od[:, j, :],
                                         start=(j == 0), stop=False)
                            for j in range(MI):
                                ins = e.matmul(bank(7)[:, C * i:C * i + C], chT[q][:, j, P * i:P * i + P], w_out[:, j, :],
                                               start=False, stop=(j == MI - 1))
                        ins.then_inc(s("o_bank"), 1)

                    def turn6(b, q):
                        e.wait_ge(s("z_ready"), B * upd[stage] + b + 1)
                        e.wait_ge(s("turn_bank_free"), B * turn[stage] + b + 2)
                        for i in range(NT):
                            ins = e.transpose(bank(6)[:, P * i:P * i + P], z[q][:, i, :], ident[:, :])
                        ins.then_inc(s("turned"), 1)
                    turn6(0, 0)
                    turn6(1, 1)
                    gates(0, 0)

                    def body(b, q):
                        states(b, q)
                        if inside(b + 1, B):
                            gates(b + 1, 1 - q)
                        outs(b, q)
                        if inside(b + 2, B):
                            turn6(b + 2, q)
                    pairs(e, body, ahead=True, behind=True)

        @block.scalar
        def _(e):
            for name, n in (("turn_bank_free", 2), ("mix_k_free", 2), ("mix_r_free", 2), ("b_free", 1)):
                e.sem_inc(s(name), n)
            if "conv" in stages:
                e.preload_act_table(ACT.Exp)
                e.wait_ge(s("conv_shift"), 1)
                for t in range(ACT_NORM, OWN):
                    ins = e.activation(y_ext[:, (REACH + t) * C:(REACH + t + 1) * C], x_blk[:, t * C:t * C + C], ACT.Identity,
                                       bias=shift_c[:, t:t + 1], scale=rstd_c[:, t:t + 1])
                ins.then_inc(s("conv_y"), 1)
                e.wait_ge(s("conv_y"), 2)

                def copy_y(n, q):
                    if inside(n - 2):
                        at(e, "yT_bank", n - 1)
                    e.copy(y_cur[q][:, :], y_ext[:, own(n, REACH * C)]).then_inc(s("y_cur"), 1)

                def copy_yT(n, q):
                    if inside(n - 2):
                        e.wait_ge(s("logits"), n - 1)
                    e.wait_ge(s("yT_bank"), n + 1)
                    e.copy(yT_cur[q][:, :], bank(q)[:, 0:P]).then_inc(s("yT_cur"), 1)

                def expo_w(n, q):
                    if inside(n - 2):
                        e.wait_ge(s("prod_vec"), n - 1)
                        e.wait_ge(s("prod_pool"), 2 * n - 2)
                    e.wait_ge(s("conv_max"), n + 1)
                    for h in range(HEADS):
                        heads = slice(h, TAPS * HEADS, HEADS)
                        ins = e.activation(e_w[q][:, heads], bank(2 + q)[:, heads], ACT.Exp, bias=mx[q][:, h:h + 1],
                                           accum_out=esum[q][:, h:h + 1])
                    ins.then_inc(s("conv_e"), 1)

                copy_y(0, 0)
                copy_y(1, 1)
                copy_yT(0, 0)
                copy_yT(1, 1)
                copy_y(2, 0)
                expo_w(0, 0)
                copy_yT(2, 0)
                copy_y(3, 1)
                expo_w(1, 1)
                copy_yT(3, 1)
                copy_y(4, 0)

                def body(n, q):
                    if inside(n + 2):
                        expo_w(n + 2, q)
                    if inside(n + 4):
                        copy_yT(n + 4, q)
                    if inside(n + 5):
                        copy_y(n + 5, 1 - q)
                pairs(e, body, ahead=3, behind=True, count=OWN)
            e.wait_ge(s("weights"), 16 * N_LOAD)
            for stage in ln_stages:
                if stage in ("ffn0", "ffn1"):
                    fb = 0 if stage == "ffn0" else B

                    def body(b, q):
                        at(e, "turned", B * turn[stage] + b + 1)
                        e.activation(xnT[:, tok(b)], bank(6 + q), ACT.Identity, bias=gam_beta[:, 1:2], scale=gam_beta[:, 0:1]) \
                            .then_inc(s("turn_bank_free"), 1)
                    pairs(e, body)
                elif stage == "attn":
                    e.preload_act_table(ACT.Exp)
                    stage_gate(e, stage)
                    nt = B * turn[stage]
                    e.wait_ge(s("zT_zero"), 2)

                    def copy_z(b, q):
                        e.wait_ge(s("turned"), nt + b + 1)
                        if not (isinstance(b, int) and b < 2):
                            e.wait_ge(s("v_bank"), b - 1)
                        e.copy(zT[q][:, 1:1 + T], bank(5)).then_inc(s("turn_bank_free"), 1)

                    def copy_coord(b, q, v):
                        e.wait_ge(s("coord_bank"), 2 * b + v + 1)
                        if not (isinstance(b, int) and b == 0) and v == 0:
                            e.wait_ge(s("lines"), b)
                        for side in range(2):
                            src = bank(5).rearrange("p (i s f) -> p i s f", i=NT, s=2)[:, :, side, :]
                            dst = coord[:, v, side * NT * HEADS:(side + 1) * NT * HEADS, 0:4].rearrange("p (i h) c -> p i h c", i=NT)
                            ins = e.copy(dst, src.rearrange("p i (h c) -> p i h c", c=4))
                        ins.then_inc(s("coord_copied"), 1)

                    def copy_v(b, q):
                        e.wait_ge(s("v_bank"), b + 1)
                        if not (isinstance(b, int) and b < 2):
                            e.wait_ge(s("weighed"), CHUNKS * (b - 1))
                        for half in range(2):
                            e.copy(v_pair[q][KB * half:KB * half + KB, :, :, 16 * half:16 * half + D_HEAD],
                                   bank(5)[KB * half:KB * half + KB, :].rearrange("p (j a d) -> p j a d", j=NJ, d=D_HEAD)) \
                                .then_inc(s("v_copied"), 1)

                    def expo_u(b, q, u):
                        g, c, i0 = u // 9, min(u % 9 // 4, 2), u % 9 % 4
                        k = 3 * g + c
                        if i0 == 0 and not (isinstance(b, int) and b == 0 and k < 3):
                            e.wait_ge(s("weighed"), CHUNKS * b + k - 2)
                        e.wait_ge(s("scored"), UNITS * b + u + 1)
                        dst = probs_c2[:, :, :].rearrange("p a b -> p (a b)") if c == 2 else probs[c][:, i0, :]
                        e.activation(dst, bank(2 * (u % 2), 2), ACT.Exp, scale=SCALE).then_inc(s("p_ready"), 1)

                    def copy_att(b):
                        e.wait_ge(s("att_turned"), b + 1)
                        if not (isinstance(b, int) and b == 0):
                            e.wait_ge(s("att_out"), b)
                        e.copy(attT[:, :], bank(6)).then_inc(s("aT_copied"), 1)

                    def guess_len(b, q):
                        e.wait_ge(s("len2"), b + 1)
                        e.activation(guess[:, :], len2[:, :], ACT.Ln, scale=4.0 ** ROOT_SHIFT)
                        e.drain()
                        e.activation(guess[:, :], guess[:, :], ACT.Exp, scale=-0.5).then_inc(s("len_guess"), 1)

                    e.preload_act_table_set("natural_log_exp_and_others")
                    copy_z(0, 0)
                    copy_coord(0, 0, 0)
                    copy_coord(0, 0, 1)
                    guess_len(0, 0)
                    e.wait_ge(s("attn_init"), 1)
                    copy_v(0, 0)

                    def body(b, q):
                        first, last = (isinstance(b, int) and b == x for x in (0, B - 1))
                        for u in range(UNITS):
                            expo_u(b, q, u)
                            if u == 6 and not first:
                                copy_att(b - 1)
                            if not last:
                                if u == 1:
                                    copy_z(b + 1, 1 - q)
                                if u in (3, 5):
                                    copy_coord(b + 1, 1 - q, (u - 3) // 2)
                                if u == 7:
                                    copy_v(b + 1, 1 - q)
                                if u == 9:
                                    guess_len(b + 1, 1 - q)
                    pairs(e, body, ahead=True, behind=True)
                    copy_att(B - 1)
                elif stage == "toep":
                    pass
                elif stage in ("mix0", "mix1"):
                    mb = 0 if stage == "mix0" else B
                    e.preload_act_table(ACT.Sigmoid)
                    stage_gate(e, stage)
                    e.wait_ge(s("zT_zero"), 2)

                    def front(b, q):
                        e.wait_ge(s("turned"), B * turn[stage] + b + 1)
                        if not (isinstance(b, int) and b < 2):
                            e.wait_ge(s("mix_xk"), mb + b - 1)
                        e.copy(zT[q][:, 1:1 + T], bank(6 + q)).then_inc(s("turn_bank_free"), 1)

                    def rest(b, q):
                        e.wait_ge(s("mix_k"), mb + b + 1)
                        if not (isinstance(b, int) and b < 2):
                            e.wait_ge(s("mix_v"), mb + b - 1)
                        e.activation(kact[q][:, :], bank(q), ACT.Relu).then_inc(s("mix_k_free"), 1)
                        e.drain()
                        e.square(kact[q][:, :], kact[q][:, :]).then_inc(s("mix_kact"), 1)
                        e.wait_ge(s("mix_r"), mb + b + 1)
                        if not (isinstance(b, int) and b < 2):
                            e.wait_ge(s("mix_gated"), mb + b - 1)
                        e.activation(rsig[q][:, :], bank(2 + q), ACT.Sigmoid).then_inc(s("mix_r_free"), 1)
                    front(0, 0)
                    front(1, 1)
                    rest(0, 0)

                    def body(b, q):
                        if inside(b + 1, B):
                            rest(b + 1, 1 - q)
                        if inside(b + 2, B):
                            front(b + 2, q)
                    pairs(e, body, ahead=True, behind=True)
                elif stage == "scan":
                    stage_gate(e, stage)
                    e.activation(decay[:, :], vecs[:, 5, :], ACT.Sigmoid, scale=-1.0).then_inc(s("scan_decay"), 1)

                    def front(b, q):
                        e.wait_ge(s("turned"), B * turn[stage] + b + 1)
                        if not (isinstance(b, int) and b < 2):
                            e.wait_ge(s("ug"), MI * (b - 1))
                        e.activation(xrT[q][:, :], bank(6), ACT.Copy, scale=norm_w[:, 0:1]).then_inc(s("turn_bank_free"), 1)

                    def gate_sig(b, q):
                        for m in range(MI):
                            e.wait_ge(s("ug"), MI * b + m + 1)
                            if not (isinstance(b, int) and b < 1):
                                e.wait_ge(s("u_ready"), MI * (b - 1) + m + 1)
                            e.activation(gate[m][:, :], bank(2 * m + 1), ACT.Sigmoid, bias=vecs[:, 1, m:m + 1]).then_inc(s("gate"), 1)

                    def b_copy(b, q):
                        for m in range(MI):
                            e.wait_ge(s("b_bank"), MI * b + m + 1)
                            if not (isinstance(b, int) and b < 1):
                                e.wait_ge(s("h_ready"), MI * (b - 1) + m + 1)
                            e.activation(bT[m][:, :], bank(4), ACT.Identity, bias=vecs[:, 2, m:m + 1]).then_inc(s("b_free"), 1)
                    front(0, 0)
                    front(1, 1)
                    gate_sig(0, 0)

                    def body(b, q):
                        b_copy(b, q)
                        if inside(b + 1, B):
                            gate_sig(b + 1, 1 - q)
                        if inside(b + 2, B):
                            front(b + 2, q)
                    pairs(e, body, ahead=True, behind=True)

        @block.vector
        def _(e):
            e.sem_inc(s("toep_bank_free"), 2)
            if "conv" in stages:
                for h in range(2):
                    for c in (2 * h, 2 * h + 1):
                        e.wait_ge(s(f"x_blk{c}"), 16)
                        for t in range(*BLOCK_CHUNKS[c]):
                            e.bn_stats(st_c[:, t, :], x_blk[:, t * C:t * C + C])
                    e.drain()
                    some = slice(h * OWN // 2, (h + 1) * OWN // 2)
                    for t in range(some.start, some.stop):
                        e.bn_aggr(mv_c[:, t, :], st_c[:, t, :])
                    e.drain()
                    e.tensor_scalar(arg_c[:, some], mv_c[:, some, 1], LN_EPS, None, ALU.add).then_inc(s("conv_var"), 1)
                e.wait_ge(s("conv_rstd"), 2)
                e.scalar_tensor_tensor(shift_c[:, :], mv_c[:, :, 0], -1.0, rstd_c[:, :], ALU.mult, ALU.mult) \
                    .then_inc(s("conv_shift"), 1)
                for t in range(ACT_NORM):
                    ins = e.tensor_scalar(y_ext[:, (REACH + t) * C:(REACH + t + 1) * C], x_blk[:, t * C:t * C + C],
                                          mv_c[:, t, 0:1], rstd_c[:, t:t + 1], ALU.subtract, ALU.mult)
                ins.then_inc(s("conv_y"), 1)

                def maximum(n, q):
                    at(e, "logits", n + 1)
                    e.tensor_reduce(mx[q][:, :], bank(2 + q)[:, 0:TAPS * HEADS].rearrange("p (k h) -> p h k", h=HEADS), AX.X, ALU.max,
                                    negate=True).then_inc(s("conv_max"), 1)

                def products(n, q):
                    e.wait_ge(s("conv_e"), n + 1)
                    at(e, "prod_free", n + 1)
                    k1 = DVE_TAPS
                    e.tensor_tensor(prod[q][:, 0:k1 * C].rearrange("p (k h r) -> p k h r", h=HEADS, r=R),
                                    y_ext[:, window(n, 0, k1)].rearrange("p (k h r) -> p k h r", h=HEADS, r=R),
                                    e_w[q][:, 0:k1 * HEADS].rearrange("p (k h) -> p k h", h=HEADS).unsqueeze(3)
                                    .to_broadcast([P, k1, HEADS, R]), ALU.mult)

                def pre_add(n, q):
                    e.reciprocal(erec[q][:, :], esum[q][:, :])
                    e.drain()
                    at(e, "prod_pool", 2 * n + 1)
                    e.tensor_tensor(prod[q][:, 0:PRE_ADDED * C], prod[q][:, 0:PRE_ADDED * C],
                                    prod[q][:, DVE_TAPS * C:(DVE_TAPS + PRE_ADDED) * C], ALU.add).then_inc(s("prod_vec"), 1)

                def average(n, q):
                    at(e, "prod_free", n + 3)
                    if inside(n - 2):
                        at(e, "conv_x", n - 1)
                    e.tensor_tensor(avg[q][:, :].rearrange("p (h r) -> p h r", r=R),
                                    bank(4 + q)[:, 0:C].rearrange("p (h r) -> p h r", r=R),
                                    erec[q][:, :].unsqueeze(2).to_broadcast([P, HEADS, R]), ALU.mult).then_inc(s("conv_avg"), 1)

                e.sem_inc(s("prod_free"), 2)
                maximum(0, 0)
                maximum(1, 1)
                e.wait_ge(s("halo"), 16 * B)

                def body(n, q):
                    if inside(n + 1):
                        products(n + 1, 1 - q)
                    if inside(n + 3):
                        maximum(n + 3, 1 - q)
                    if inside(n - 1):
                        average(n - 1, 1 - q)
                        e.drain()
                    if inside(n + 1):
                        pre_add(n + 1, 1 - q)
                body(-1, 1)
                pairs(e, body, ahead=2, behind=True, count=OWN)
                average(OWN - 1, 1)

            e.wait_ge(s("weights"), 16 * N_LOAD)
            if "ffn0" in stages:
                e.tensor_reduce(w_beta[:, 0:1], w_raw[:, :], AX.X, ALU.add, apply_absolute_value=True).then_inc(s("w_abs"), 1)
                e.wait_ge(s("w_mean"), 1)
                e.tensor_copy(w_beta[:, 1:2], bank(5)[:, 0:1])
                e.drain()
                e.tensor_scalar(w_beta[:, 2:3], w_beta[:, 1:2], LN_EPS, None, ALU.add)
                e.drain()
                e.tensor_scalar(w_beta[:, 2:3], w_beta[:, 2:3], 0.5, None, ALU.mult)
                e.drain()
                e.tensor_scalar(w_beta[:, 3:4], w_beta[:, 2:3], -1.0, None, ALU.mult)
                e.tensor_scalar(w_q[:, :], w_raw[:, :], w_beta[:, 2:3], None, ALU.is_gt)
                e.drain()
                e.tensor_scalar(w_scr[:, :], w_raw[:, :], w_beta[:, 3:4], None, ALU.is_lt)
                e.drain()
                e.tensor_tensor(w_q[:, :], w_q[:, :], w_scr[:, :], ALU.subtract)
                e.drain()

            for stage in ln_stages:
                fac, add = LN_CONST[kind[stage]]
                if stage in ("ffn0", "ffn1"):
                    fb = 0 if stage == "ffn0" else B
                    ln_stats(e, stage, 0, 0, fac, add)
                    ln_stats(e, stage, 1, 1, fac, add)
                    ln_norm(e, stage, 0, 0)
                    ln_norm(e, stage, 1, 1)

                    def body(b, q):
                        if inside(b + 2, B):
                            ln_stats(e, stage, b + 2, q, fac, add)
                        at(e, "turn_bank_free", B * turn[stage] + b + 3)
                        dst = amax[:, b:b + 1] if isinstance(b, int) else amax[:, bass.ds(b, 1)]
                        e.tensor_reduce(dst, xnT[:, tok(b)], AX.X, ALU.max, apply_absolute_value=True)
                        if inside(b + 2, B):
                            ln_norm(e, stage, b + 2, q)
                    pairs(e, body, ahead=True)
                    e.drain()
                    e.tensor_reduce(amax1[:, :], amax[:, :], AX.X, ALU.max).then_inc(s("amax"), 1)
                    e.wait_ge(s("gmax"), 1 if stage == "ffn0" else 2)
                    e.tensor_scalar(bound[:, 0:1], gmax[:, :], CLIP, None, ALU.mult)
                    e.tensor_scalar(bound[:, 1:2], gmax[:, :], -CLIP, None, ALU.mult)
                    e.drain()

                    def clip(b, q):
                        if not (isinstance(b, int) and b < 2):
                            at(e, "ffn_y", fb + b - 1)
                        e.tensor_scalar(clipped[q][:, :], xnT[:, tok(b)], bound[:, 0:1], bound[:, 1:2], ALU.min, ALU.max) \
                            .then_inc(s("clipped"), 1)

                    def add_y(b, q):
                        at(e, "ffn_y", fb + b + 1)
                        e.scalar_tensor_tensor(x_tile[:, tok(b)], bank(q), w_beta[:, 1:2], x_tile[:, tok(b)], ALU.mult, ALU.add) \
                            .then_inc(s("x_updated"), 1)
                    clip(0, 0)
                    clip(1, 1)

                    def body(b, q):
                        add_y(b, q)
                        if not (isinstance(b, int) and b >= B - 2):
                            clip(b + 2, q)
                    pairs(e, body, ahead=True)
                elif stage == "attn":
                    stage_gate(e, stage)
                    e.tensor_copy(b_v_wide[:, :], b_v[:, 0:1].to_broadcast([P, P]))
                    e.tensor_copy(ident_b[:, :], ident[:, :])
                    e.drain().then_inc(s("b_v_wide"), 1)
                    ln_stats(e, stage, 0, 0, fac, add)
                    e.wait_ge(s("bias_bank"), 1)
                    e.tensor_copy(att_bias[:, :], bank(4)[:, 0:C]).then_inc(s("att_bias"), 1)
                    ln_norm(e, stage, 0, 0)
                    ln_stats(e, stage, 1, 1, fac, add)

                    def lines(b, q):
                        e.wait_ge(s("coord_copied"), 2 * b + 2)
                        e.tensor_copy(coord[:, :, :, 4:6].rearrange("p v g c -> p (v g) c"), coord[:, :, :, 1:3].rearrange("p v g c -> p (v g) c"))
                        pa, pb = (coord[:, v, :, :].rearrange("p (s g) c -> p s g c", s=2) for v in range(2))
                        shape = [P, 2, NT * HEADS, 3]

                        def star(m):
                            return triple(m, 0, 3)

                        def tri(m):
                            return triple(m, 3, -3)

                        def triple(m, start, shift):
                            v = m[:, :, :, start:start + 3]
                            (ps_, pn), (ss, sn), (gs, gn), (cs, cn) = v.ap
                            return bass.AP(v.tensor, v.offset, [[ps_, pn], [ss + shift, sn], [gs, gn], [cs, cn]])
                        e.tensor_tensor(star(m_a), pa[:, :, :, 0:1].to_broadcast(shape), pb[:, :, :, 1:4], ALU.mult)
                        e.tensor_tensor(star(m_b), pb[:, :, :, 0:1].to_broadcast(shape), pa[:, :, :, 1:4], ALU.mult)
                        e.drain()
                        e.tensor_tensor(tri(m_a), pa[:, :, :, 2:5], pb[:, :, :, 3:6], ALU.mult)
                        e.tensor_tensor(tri(m_b), pb[:, :, :, 2:5], pa[:, :, :, 3:6], ALU.mult)
                        e.drain().then_inc(s("lines"), 1)
                        e.tensor_tensor(line[:, :, :, :], m_a[:, :, :, :], m_b[:, :, :, :], ALU.subtract)
                        e.drain()
                        e.tensor_tensor(m_a[:, :, :, :], line[:, :, :, :], line[:, :, :, :], ALU.mult)
                        e.drain()
                        e.tensor_reduce(len2[:, :], m_a[:, :, :, :].rearrange("p s g c -> p (s g) c"), AX.X, ALU.add)
                        e.drain()
                        e.tensor_scalar(len2[:, :], len2[:, :], 1e-24, None, ALU.max).then_inc(s("len2"), 1)

                    def split(b, q):
                        e.wait_ge(s("inv_len"), b + 1)
                        lv = line[:, :, :, :].rearrange("p s g c -> p (s g) c")
                        e.tensor_tensor(lv, lv, inv_len[:, :].unsqueeze(2).to_broadcast([P, 2 * NT * HEADS, COMPS]), ALU.mult)
                        e.drain()
                        if not (isinstance(b, int) and b == 0):
                            e.wait_ge(s("qk_turned"), PAIRS * b)
                        sides = ((split_q, slice(0, 3), slice(3, 5), 5), (split_k, slice(1, 6, 2), slice(2, 5, 2), 0))
                        sv = [sp[:, :, 0:SLOTS * COMPS].rearrange("p g (t c) -> p g t c", c=COMPS) for sp, *_ in sides]
                        for n, (sp, hs, ms, ls) in enumerate(sides):
                            e.tensor_copy(sv[n][:, :, hs, :], line[:, n, :, :].unsqueeze(2).to_broadcast([P, NT * HEADS, 3, COMPS]))
                        e.drain()
                        for n, (sp, hs, ms, ls) in enumerate(sides):
                            e.tensor_tensor(rest[:, n, :, :], line[:, n, :, :], sv[n][:, :, 1, :], ALU.subtract)
                        e.drain()
                        for n, (sp, hs, ms, ls) in enumerate(sides):
                            e.tensor_copy(sv[n][:, :, ms, :], rest[:, n, :, :].unsqueeze(2).to_broadcast([P, NT * HEADS, 2, COMPS]))
                        e.drain()
                        for n, (sp, hs, ms, ls) in enumerate(sides):
                            e.tensor_tensor(sv[n][:, :, ls, :], rest[:, n, :, :], sv[n][:, :, 4, :], ALU.subtract).then_inc(s("split"), 1)

                    def copy_qk(b, q, r):
                        e.wait_ge(s("qk_turned"), PAIRS * b + r + 1)
                        src = bank(7).bitcast(BF16)
                        e.tensor_copy(qT[q][0:QK_ROWS, r, :], src[0:QK_ROWS, 0:T])
                        for half in range(2):
                            rows = slice(ROWS_B * half, ROWS_B * half + SLOTS * COMPS)
                            ins = e.tensor_copy(kT[q][rows, r, :, KB * half:KB * half + KB],
                                                src[rows, T:2 * T].rearrange("p (j t) -> p j t", t=KB))
                        ins.then_inc(s("qk_copied"), 1)

                    def copy_pv(b, g):
                        e.wait_ge(s("weighed"), CHUNKS * b + 3 * g + 3)
                        if not (isinstance(b, int) and b == 0 and g == 0):
                            e.wait_ge(s("pv_turned"), 2 * b + g)
                        e.tensor_copy(pv_sb[:, :], bank(4)).then_inc(s("pv_copied"), 1)

                    def norm_att(b, g):
                        e.drain()
                        e.wait_ge(s("pv_turned"), 2 * b + g + 1)
                        pv = bank(6).rearrange("p (i h v) -> p i h v", i=NT, v=16)
                        e.reciprocal(inv_den[:, :, :], pv[:, :, :, D_HEAD])
                        e.drain()
                        if g == 0 and not (isinstance(b, int) and b == 0):
                            e.wait_ge(s("att_turned"), b)
                        for i in range(NT):
                            ins = e.tensor_tensor(att[:, i, 64 * g:64 * g + 64].rearrange("p (h v) -> p h v", v=D_HEAD), pv[:, i, :, 0:D_HEAD],
                                                  inv_den[:, i, :].unsqueeze(2).to_broadcast([P, 8, D_HEAD]), ALU.mult)
                        ins.then_inc(s("att_ready"), 1)

                    def add_att(b):
                        e.wait_ge(s("x_biased"), b + 1)
                        at(e, "att_out", b + 1)
                        e.tensor_tensor(x_tile[:, tok(b)], bank(6), x_tile[:, tok(b)], ALU.add).then_inc(s("x_updated"), 1)

                    lines(0, 0)
                    ln_norm(e, stage, 1, 1)
                    e.wait_ge(s("attn_init"), 1)
                    split(0, 0)
                    copy_qk(0, 0, 0)
                    copy_qk(0, 0, 1)

                    def body(b, q):
                        first, last = (isinstance(b, int) and b == x for x in (0, B - 1))
                        for r in (2, 3, 4):
                            copy_qk(b, q, r)
                        if not first:
                            copy_pv(b - 1, 1)
                        copy_qk(b, q, 5)
                        copy_qk(b, q, 6)
                        if not first:
                            norm_att(b - 1, 1)
                        copy_qk(b, q, 7)
                        if not last:
                            lines(b + 1, 1 - q)
                        if not first:
                            add_att(b - 1)
                        if not (isinstance(b, int) and b >= B - 2):
                            ln_stats(e, stage, b + 2, q, fac, add)
                        copy_pv(b, 0)
                        if not last:
                            split(b + 1, 1 - q)
                            copy_qk(b + 1, 1 - q, 0)
                        norm_att(b, 0)
                        if not last:
                            copy_qk(b + 1, 1 - q, 1)
                        if not (isinstance(b, int) and b >= B - 2):
                            ln_norm(e, stage, b + 2, q)
                    pairs(e, body, ahead=True, behind=True)
                    copy_pv(B - 1, 1)
                    norm_att(B - 1, 1)
                    add_att(B - 1)
                elif stage == "toep":
                    stage_gate(e, stage)
                    e.wait_ge(s("kernel_bank"), 1)
                    for v in range(3):
                        src = bank(v).rearrange("p (h w c) -> p h w c", h=2, w=2)
                        e.tensor_copy(kf[0][:, v, :, :], src[:, :, 0, :])
                        e.drain()
                        ins = e.scalar_tensor_tensor(kf[1][:, v, :, :], kf[0][:, v, :, :], sgn[:, 0:1], src[:, :, 1, :], ALU.mult, ALU.add)
                    ins.then_inc(s("kernel_ready"), 1)
                    e.drain()
                    ln_stats(e, stage, 0, 0, fac, add)
                    ln_norm(e, stage, 0, 0)

                    def body(b, q):
                        last = isinstance(b, int) and b == B - 1
                        if not last:
                            ln_stats(e, stage, b + 1, 1 - q, fac, add)
                        e.drain()
                        e.wait_ge(s("toep_z_used"), b + 1)
                        re, im = (bank(2 * q + v).rearrange("p (h w c) -> p h w c", h=2, w=2) for v in range(2))

                        def k0(v):
                            return kf[0][:, v, :, :].unsqueeze(2).to_broadcast([P, 2, 2, C])
                        for n, (src, v) in enumerate(((re, 0), (im, 1), (re, 1), (im, 2))):
                            ins = e.tensor_tensor(pu[n][:, :, :], src[:, :, 0, :], kf[1][:, v, :, :], ALU.mult)
                        ins.then_inc(s("toep_pu"), 1)
                        for n, (src, v) in enumerate(((re, 0), (im, 1), (re, 1), (im, 2))):
                            ins = e.tensor_tensor(pr[n][:, :, :, :], src, k0(v), ALU.mult)
                        ins.then_inc(s("toep_bank_free"), 1)
                        if not last:
                            ln_norm(e, stage, b + 1, 1 - q)
                        e.drain()
                        if not (isinstance(b, int) and b < 2):
                            e.wait_ge(s("toep_out"), b - 1)
                        e.tensor_tensor(yf[q][:, 0, :, :, :], pr[0][:, :, :, :], pr[1][:, :, :, :], ALU.subtract)
                        e.tensor_tensor(yf[q][:, 1, :, :, :], pr[2][:, :, :, :], pr[3][:, :, :, :], ALU.add)
                        e.drain()
                        e.wait_ge(s("toep_cross"), b + 1)
                        e.tensor_tensor(yf[q][:, 0, :, 1, :], yf[q][:, 0, :, 1, :], pu[0][:, :, :], ALU.add)
                        e.tensor_tensor(yf[q][:, 1, :, 1, :], yf[q][:, 1, :, 1, :], pu[2][:, :, :], ALU.add).then_inc(s("toep_spec"), 1)
                        if not (isinstance(b, int) and b == 0):
                            res(b - 1, 1 - q)

                    def res(b, q):
                        at(e, "toep_out", b + 1)
                        xv = x_tile[:, tok(b)].rearrange("p (w k c) -> p k w c", w=2, k=2)
                        e.tensor_tensor(xv, bank(4 + q).rearrange("p (k w c) -> p k w c", w=2, k=2), xv, ALU.add) \
                            .then_inc(s("x_updated"), 1)
                    pairs(e, body, ahead=True, behind=True)
                    res(B - 1, 1)
                elif stage in ("mix0", "mix1"):
                    mb = 0 if stage == "mix0" else B
                    ln_stats(e, stage, 0, 0, fac, add)
                    ln_stats(e, stage, 1, 1, fac, add)
                    ln_norm(e, stage, 0, 0)
                    ln_norm(e, stage, 1, 1)

                    def mix(b, q):
                        e.wait_ge(s("turn_bank_free"), B * turn[stage] + b + 3)
                        e.tensor_tensor(dif[q][:, :], zT[q][:, 1:1 + T], zT[q][:, 0:T], ALU.subtract)
                        e.drain()
                        if not (isinstance(b, int) and b < 2):
                            e.wait_ge(s("mix_r"), mb + b - 1)
                        e.scalar_tensor_tensor(xrT[q][:, :], dif[q][:, :], mus[:, 0:1], zT[q][:, 0:T], ALU.mult, ALU.add)
                        e.scalar_tensor_tensor(xkT[q][:, :], dif[q][:, :], mus[:, 1:2], zT[q][:, 0:T], ALU.mult, ALU.add) \
                            .then_inc(s("mix_xk"), 1)

                    def gated_v(b, q):
                        e.wait_ge(s("mix_v"), mb + b + 1)
                        e.wait_ge(s("mix_r_free"), mb + b + 3)
                        if not (isinstance(b, int) and b < 2):
                            e.wait_ge(s("x_updated"), B * upd[stage] + b - 1)
                        e.tensor_tensor(gated[q][:, :], bank(4 + q), rsig[q][:, :], ALU.mult).then_inc(s("mix_gated"), 1)

                    mix(0, 0)

                    def body(b, q):
                        if inside(b + 2, B):
                            ln_stats(e, stage, b + 2, q, fac, add)
                        if inside(b + 1, B):
                            mix(b + 1, 1 - q)
                        gated_v(b, q)
                        if inside(b + 2, B):
                            ln_norm(e, stage, b + 2, q)
                    pairs(e, body, ahead=True, behind=True)
                elif stage == "scan":
                    stage_gate(e, stage)
                    ln_stats(e, stage, 0, 0, fac, add, extra=True)
                    ln_norm(e, stage, 0, 0)
                    for j in range(MI):
                        e.memset(decay_row[:, j, 0:2 * P], 1.0)
                    e.drain()
                    for j in range(MI):
                        ins = e.tensor_scalar(decay_row[:, j, 0:P], decay_row[:, j, 0:P], vecs[:, 4, j:j + 1], None, ALU.mult)
                    ins.then_inc(s("scan_const"), 1)
                    e.wait_ge(s("scan_fold"), 1)
                    e.tensor_copy(w_od[:, :, :].rearrange("p m c -> p (m c)"), bank(5)[:, 0:MI * C])
                    e.tensor_copy(bias_row[:, :], bank(4)[:, 0:C])
                    for j in range(MI):
                        e.memset(decay_row[:, j, :], 1.0)
                    e.drain()
                    e.wait_ge(s("scan_decay"), 1)
                    for j in range(MI):
                        ins = e.tensor_scalar(decay_row[:, j, :], decay_row[:, j, :], decay[:, j:j + 1], None, ALU.mult)
                    ins.then_inc(s("scan_ready"), 1)
                    e.drain()

                    def u_mul(b, q):
                        for m in range(MI):
                            e.wait_ge(s("gate"), MI * b + m + 1)
                            if not (isinstance(b, int) and b < 2):
                                e.wait_ge(s("o_bank"), b - 1)
                            e.scalar_tensor_tensor(uT[q][:, m, :], bank(2 * m), vecs[:, 0, m:m + 1], gate[m][:, :], ALU.add, ALU.mult) \
                                .then_inc(s("u_ready"), 1)

                    def first(b, q):
                        e.wait_ge(s("ratio"), b + 1)
                        e.wait_ge(s("z_ready"), B * upd[stage] + b + 1)
                        for i in range(NT):
                            e.scalar_tensor_tensor(x_plus[q][:, i * C:i * C + C], z[q][:, i, :], rstd[q][:, 1, i:i + 1],
                                                   bias_row[:, :], ALU.mult, ALU.add)

                    def h_scan(b, q):
                        for m in range(MI):
                            e.wait_ge(s("b_free"), MI * b + m + 1 + 1)
                            e.tensor_tensor_scan(hT[m][:, :], decay_row[:, m, :], bT[m][:, :], 0.0, ALU.mult, ALU.add) \
                                .then_inc(s("h_ready"), 1)
                            e.drain()
                            e.wait_ge(s("c_bank"), MI * b + m + 1)
                            if not (isinstance(b, int) and b < 2):
                                e.wait_ge(s("o_bank"), b - 1)
                            e.scalar_tensor_tensor(chT[q][:, m, :], bank(5), vecs[:, 3, m:m + 1], hT[m][:, :], ALU.add, ALU.mult) \
                                .then_inc(s("ch_ready"), 1)

                    def res(b, q):
                        e.tensor_tensor(x_plus[q][:, :], x_plus[q][:, :], x_tile[:, tok(b)], ALU.add)
                        e.drain()
                        at(e, "o_bank", b + 1)
                        e.tensor_tensor(x_tile[:, tok(b)], bank(7), x_plus[q][:, :], ALU.add).then_inc(s("x_updated"), 1)

                    ln_stats(e, stage, 1, 1, fac, add, extra=True)
                    ln_norm(e, stage, 1, 1)
                    u_mul(0, 0)
                    first(0, 0)

                    def body(b, q):
                        if inside(b + 2, B):
                            ln_stats(e, stage, b + 2, q, fac, add, extra=True)
                        h_scan(b, q)
                        if inside(b + 1, B):
                            u_mul(b + 1, 1 - q)
                            first(b + 1, 1 - q)
                        if inside(b + 2, B):
                            ln_norm(e, stage, b + 2, q)
                        res(b, q)
                    pairs(e, body, ahead=True, behind=True)


def dft_tables():
    n = 2 * WIN
    t = np.arange(WIN)[:, None]
    f = np.arange(WIN)[None, :]
    ang = 2 * np.pi * ((t * f) % n) / n
    cos, sin = np.cos(ang), np.sin(ang)
    nyq = np.cos(np.pi * t)
    sin_n, cos_n = sin.copy(), cos.copy()
    sin_n[:, 0:1] = nyq
    cos_n[:, 0:1] = nyq
    fwd = np.concatenate([cos, sin_n, sin[:, :P], cos_n[:, :P]], axis=1)
    fwd = fwd.reshape(2, P, 6 * P).transpose(1, 0, 2)
    wgt = np.full((WIN, 1), 2.0 / n)
    wgt[0] = 1.0 / n
    inv = np.concatenate([cos.T * wgt, sin_n.T * wgt], axis=0)
    inv = inv.reshape(4, P, WIN).transpose(1, 0, 2)
    return np.ascontiguousarray(fwd, np.float32), np.ascontiguousarray(inv, np.float32)


def build(nc, arrays, stages=STAGES):
    d = {}
    for name, a in arrays.items():
        d[name] = nc.dram_tensor(f"in_{name}", a.shape, mybir.dt.from_np(a.dtype), kind="ExternalInput").ap()
    out = nc.dram_tensor("out_x", (B * T, C), F32, kind="ExternalOutput").ap()
    program(nc, d, out, stages)


def lay_out(i):
    g = {k: np.asarray(v) for k, v in i.items()}
    c = np.ascontiguousarray

    def by_tile(v):
        return v.reshape(MI, P).T
    fwd, inv = dft_tables()
    expo = np.empty((P, 3, NT), np.float32)
    expo[:, 0], expo[:, 1], expo[:, 2] = -0.5, 0.5, -0.5
    return {
        "x": g["L0_attn_a_x"].reshape(P, OWN * C),
        "ident": np.eye(P, dtype=np.float32),
        "w_lin": c(g["L0_attn_a_w_lin"].reshape(HEADS, TAPS, C).transpose(2, 1, 0).reshape(C, TAPS * HEADS)),
        "gam_beta": c(np.stack([g["L0_ffn_ln_gamma"], g["L0_ffn_ln_beta"]], 1)),
        "weight": g["L0_ffn_weight"],
        "dft_f": fwd, "dft_i": inv,
        "sgn": np.where(np.arange(P) % 2 == 0, 1.0, -1.0).astype(np.float32)[:, None],
        "t": c(g["L1_attn_a_t"].reshape(NT, P, C).transpose(1, 0, 2)),
        "W_r": c(g["L1_ffn_W_r"].T), "W_k": c(g["L1_ffn_W_k"].T), "W_v": c(g["L1_ffn_W_v"].T),
        "mus": c(np.stack([g["L1_ffn_mu_r"], g["L1_ffn_mu_k"]], 1)),
        "in_w": c(g["L1_attn_b_in_w"].T), "gate_w": c(g["L1_attn_b_gate_w"].T),
        "b_w": c(g["L1_attn_b_b_w"].T.reshape(MI, P, INNER).transpose(1, 0, 2)),
        "c_w": c(g["L1_attn_b_c_w"].T.reshape(MI, P, INNER).transpose(1, 0, 2)),
        "d_w": c(g["L1_attn_b_d_w"].reshape(MI, P, INNER).transpose(1, 0, 2)),
        "out_w": c(g["L1_attn_b_out_w"].T.reshape(MI, P, C).transpose(1, 0, 2)),
        "vecs": c(np.stack([by_tile(g["L1_attn_b_" + n]) for n in ("in_b", "gate_b", "b_b", "c_b", "d_b", "a_log")], 1)),
        "norm_w": c(g["L1_attn_b_norm_w"][:, None]),
        "out_b": c(g["L1_attn_b_out_b"][None, :]),
        "expo": expo,
        "w_qk": c(np.stack([np.concatenate([g["L0_attn_b_W1_q"][:C], g["L0_attn_b_W1_k"]], 1),
                            np.concatenate([g["L0_attn_b_W2_q"][:C], g["L0_attn_b_W2_k"]], 1)], 1)),
        "w_qp": c(np.stack([g["L0_attn_b_W1_q"][C:], g["L0_attn_b_W2_q"][C:]], 1)),
        "w_val": c(g["L0_attn_b_W_v"].reshape(C, PAIRS, 2, D_HEAD).transpose(0, 2, 1, 3).reshape(C, C)),
        "W_o": g["L0_attn_b_W_o"], "b_v": c(g["L0_attn_b_b_v"][:, None]), "b_o": c(g["L0_attn_b_b_o"][None, :]),
        "mask": (np.arange(KB)[None, :] >= (np.arange(P) % KB)[:, None]).astype(np.float32),
    }


def kernel(**inputs):
    import concourse.bacc as _bacc
    from concourse.bass_utils import run_bass_kernel_spmd as _run

    arrays = lay_out(inputs)
    nc = _bacc.Bacc("TRN2", target_bir_lowering=False, num_devices=1)
    build(nc, arrays)
    r = _run(nc, [{f"in_{k}": v for k, v in arrays.items()}], core_ids=[0])
    return r.results[0]["out_x"].reshape(B, T, C)
```
